# Optimizing a Trainium2 kernel written in Bass

```python
import numpy as np
import jax
import jax.numpy as jnp

def _softmax(x, axis=-1):
    return jax.nn.softmax(x, axis=axis)

def _gelu(x):
    return jax.nn.gelu(x, approximate=True)

def _silu(x):
    return jax.nn.silu(x)

def _sigmoid(x):
    return jax.nn.sigmoid(x)

def _layernorm(x, axis=-1, eps=1e-05):
    m = jnp.mean(x, axis=axis, keepdims=True)
    v = jnp.var(x, axis=axis, keepdims=True)
    return (x - m) / jnp.sqrt(v + eps)

def _scatter_add(tgt, idx, src, axis=0):
    return tgt.at[idx].add(src)

def _segment_sum(src, seg, n):
    return jax.ops.segment_sum(src, seg, n)
kernel_name = 'mk_adj_resnorm_d4_adj_r2_918bee'

def setup_inputs(seed: int=0):
    np.random.seed(seed)
    _w = jnp.asarray

    def _rec_inputs():
        import jax
        import jax.numpy as jnp
        _gk = jax.random.key(seed)
        x = -0.0002928 + 1 * jax.random.normal(jax.random.fold_in(_gk, 1), (32, 256, 128), jnp.float32)
        _a = jax.random.bernoulli(jax.random.fold_in(_gk, 2), 0.0078125, (32, 256, 256))
        _a = jnp.logical_or(_a, jnp.swapaxes(_a, -1, -2))
        _a = jnp.logical_or(_a, jnp.eye(256, dtype=bool))
        _af = _a.astype(jnp.float32)
        _af = _af * jax.random.uniform(jax.random.fold_in(_gk, 3), (32, 256, 256), jnp.float32, 0.05, 0.999995)
        adj = _af
        return (x, adj)
    x, adj = _rec_inputs()

    def _L0_gnn_setup():
        import jax, jax.numpy as jnp
        import numpy as np
        B, N, D = (4, 2048, 128)
        DENSITY = 0.02
        key = jax.random.key(seed)
        kx, ka1, ka2, kwt, kbt, kwh, kth = jax.random.split(key, 7)
        x = jax.random.normal(kx, (B, N, D), dtype=jnp.float32)
        mask = jax.random.uniform(ka1, (B, N, N)) < DENSITY
        vals = jax.random.uniform(ka2, (B, N, N), dtype=jnp.float32)
        adj = jnp.where(mask, vals, 0.0).astype(jnp.float32)
        s = 0.02
        W_t = s * jax.random.normal(kwt, (D, D), dtype=jnp.float32)
        b_t = s * jax.random.normal(kbt, (D,), dtype=jnp.float32)
        W_h = s * jax.random.normal(kwh, (D, D), dtype=jnp.float32)
        theta = s * jax.random.normal(kth, (D, D), dtype=jnp.float32)
        return {'x': x, 'adj': adj, 'W_t': W_t, 'b_t': b_t, 'W_h': W_h, 'theta': theta}
    _L0_gnn_all = _L0_gnn_setup()
    _L0_gnn_in = {k: v for k, v in _L0_gnn_all.items() if k in ('W_t', 'b_t', 'W_h', 'theta')}
    del _L0_gnn_all

    def _L1_gnn_setup():
        import jax, jax.numpy as jnp
        import numpy as np
        D_IN = 128
        D_HID = 256
        key = jax.random.key(seed)
        k1, k2, k3, k4, k5, k6 = jax.random.split(key, 6)
        x = jax.random.normal(k1, (8, 2048, D_IN), dtype=jnp.float32)
        adj = jax.random.uniform(k2, (8, 2048, 2048), dtype=jnp.float32)
        s1 = 1.0 / np.sqrt(D_IN)
        s2 = 1.0 / np.sqrt(D_HID)
        W1 = jax.random.uniform(k3, (D_IN, D_HID), dtype=jnp.float32, minval=-s1, maxval=s1)
        b1 = jax.random.uniform(k4, (D_HID,), dtype=jnp.float32, minval=-s1, maxval=s1)
        W2 = jax.random.uniform(k5, (D_HID, D_IN), dtype=jnp.float32, minval=-s2, maxval=s2)
        b2 = jax.random.uniform(k6, (D_IN,), dtype=jnp.float32, minval=-s2, maxval=s2)
        eps = jnp.zeros((1,), dtype=jnp.float32)
        return {'x': x, 'adj': adj, 'eps': eps, 'W1': W1, 'b1': b1, 'W2': W2, 'b2': b2}
    _L1_gnn_all = _L1_gnn_setup()
    _L1_gnn_in = {k: v for k, v in _L1_gnn_all.items() if k in ('eps', 'W1', 'b1', 'W2', 'b2')}
    del _L1_gnn_all

    def _L2_gnn_setup():
        import jax, jax.numpy as jnp
        import numpy as np
        from jax import lax
        DIM = 128
        EPS = 1e-05

        def _bn(h, g, b, m, v):
            scale = g / jnp.sqrt(v + EPS)
            return h * scale[None, :, None] + (b - m * scale)[None, :, None]

        def _conv1d(h, w, pad):
            return lax.conv_general_dilated(h, w, window_strides=(1,), padding=[(pad, pad)], dimension_numbers=('NCH', 'OIH', 'NCH'))
        key = jax.random.key(seed)
        ks = jax.random.split(key, 16)
        bs, n, d = (16, 1024, DIM)
        s = 0.05
        return {'x': jax.random.normal(ks[0], (bs, n, d), jnp.float32), 'mask': jnp.ones((bs, n, n), jnp.float32), 'w_se': jax.random.normal(ks[1], (3, d), jnp.float32) * s, 'b_se': jnp.zeros((3,), jnp.float32), 'conv1_w': jax.random.normal(ks[2], (d, d, 1), jnp.float32) * s, 'bn1_g': jnp.ones((d,), jnp.float32), 'bn1_b': jnp.zeros((d,), jnp.float32), 'bn1_m': jnp.zeros((d,), jnp.float32), 'bn1_v': jnp.ones((d,), jnp.float32), 'conv2_w': jax.random.normal(ks[3], (d, d, 17), jnp.float32) * s, 'bn2_g': jnp.ones((d,), jnp.float32), 'bn2_b': jnp.zeros((d,), jnp.float32), 'bn2_m': jnp.zeros((d,), jnp.float32), 'bn2_v': jnp.ones((d,), jnp.float32), 'w_msg': jax.random.normal(ks[4], (d, d), jnp.float32) * s, 'b_msg': jnp.zeros((d,), jnp.float32), 'w_ih': jax.random.normal(ks[5], (3 * d, 2 * d), jnp.float32) * s, 'b_ih': jnp.zeros((3 * d,), jnp.float32), 'w_hh': jax.random.normal(ks[6], (3 * d, d), jnp.float32) * s, 'b_hh': jnp.zeros((3 * d,), jnp.float32)}
    _L2_gnn_all = _L2_gnn_setup()
    _L2_gnn_in = {k: v for k, v in _L2_gnn_all.items() if k in ('w_se', 'b_se', 'conv1_w', 'bn1_g', 'bn1_b', 'bn1_m', 'bn1_v', 'conv2_w', 'bn2_g', 'bn2_b', 'bn2_m', 'bn2_v', 'w_msg', 'b_msg', 'w_ih', 'b_ih', 'w_hh', 'b_hh')}
    del _L2_gnn_all

    def _L3_gnn_setup():
        import math
        import jax, jax.numpy as jnp
        import numpy as np
        B, N, D, H = (32, 256, 128, 8)
        HD = D // H
        key = jax.random.key(seed)
        ks = jax.random.split(key, 9)
        h = jax.random.normal(ks[0], (B, N, D), dtype=jnp.float32)
        edge = jax.random.normal(ks[1], (B, N, N), dtype=jnp.float32)
        adj = jax.random.uniform(ks[2], (B, N, N)) < 0.5
        adj_mask = adj | jnp.eye(N, dtype=bool)[None]
        s = 1.0 / math.sqrt(D)
        W_q = jax.random.normal(ks[3], (D, D), dtype=jnp.float32) * s
        W_k = jax.random.normal(ks[4], (D, D), dtype=jnp.float32) * s
        W_v = jax.random.normal(ks[5], (D, D), dtype=jnp.float32) * s
        W_e = jax.random.normal(ks[6], (H, 1), dtype=jnp.float32)
        W_o = jax.random.normal(ks[7], (D, D), dtype=jnp.float32) * s
        return {'h': h, 'edge': edge, 'adj_mask': adj_mask, 'W_q': W_q, 'W_k': W_k, 'W_v': W_v, 'W_e': W_e, 'W_o': W_o}
    _L3_gnn_all = _L3_gnn_setup()
    _L3_gnn_in = {k: v for k, v in _L3_gnn_all.items() if k in ('W_q', 'W_k', 'W_v', 'W_e', 'W_o')}
    del _L3_gnn_all
    return {'x': x, 'adj': adj, 'L0_gnn_W_t': _L0_gnn_in['W_t'], 'L0_gnn_b_t': _L0_gnn_in['b_t'], 'L0_gnn_W_h': _L0_gnn_in['W_h'], 'L0_gnn_theta': _L0_gnn_in['theta'], 'L1_gnn_eps': _L1_gnn_in['eps'], 'L1_gnn_W1': _L1_gnn_in['W1'], 'L1_gnn_b1': _L1_gnn_in['b1'], 'L1_gnn_W2': _L1_gnn_in['W2'], 'L1_gnn_b2': _L1_gnn_in['b2'], 'L2_gnn_w_se': _L2_gnn_in['w_se'], 'L2_gnn_b_se': _L2_gnn_in['b_se'], 'L2_gnn_conv1_w': _L2_gnn_in['conv1_w'], 'L2_gnn_bn1_g': _L2_gnn_in['bn1_g'], 'L2_gnn_bn1_b': _L2_gnn_in['bn1_b'], 'L2_gnn_bn1_m': _L2_gnn_in['bn1_m'], 'L2_gnn_bn1_v': _L2_gnn_in['bn1_v'], 'L2_gnn_conv2_w': _L2_gnn_in['conv2_w'], 'L2_gnn_bn2_g': _L2_gnn_in['bn2_g'], 'L2_gnn_bn2_b': _L2_gnn_in['bn2_b'], 'L2_gnn_bn2_m': _L2_gnn_in['bn2_m'], 'L2_gnn_bn2_v': _L2_gnn_in['bn2_v'], 'L2_gnn_w_msg': _L2_gnn_in['w_msg'], 'L2_gnn_b_msg': _L2_gnn_in['b_msg'], 'L2_gnn_w_ih': _L2_gnn_in['w_ih'], 'L2_gnn_b_ih': _L2_gnn_in['b_ih'], 'L2_gnn_w_hh': _L2_gnn_in['w_hh'], 'L2_gnn_b_hh': _L2_gnn_in['b_hh'], 'L3_gnn_W_q': _L3_gnn_in['W_q'], 'L3_gnn_W_k': _L3_gnn_in['W_k'], 'L3_gnn_W_v': _L3_gnn_in['W_v'], 'L3_gnn_W_e': _L3_gnn_in['W_e'], 'L3_gnn_W_o': _L3_gnn_in['W_o']}

def reference(x, adj, L0_gnn_W_t, L0_gnn_b_t, L0_gnn_W_h, L0_gnn_theta, L1_gnn_eps, L1_gnn_W1, L1_gnn_b1, L1_gnn_W2, L1_gnn_b2, L2_gnn_w_se, L2_gnn_b_se, L2_gnn_conv1_w, L2_gnn_bn1_g, L2_gnn_bn1_b, L2_gnn_bn1_m, L2_gnn_bn1_v, L2_gnn_conv2_w, L2_gnn_bn2_g, L2_gnn_bn2_b, L2_gnn_bn2_m, L2_gnn_bn2_v, L2_gnn_w_msg, L2_gnn_b_msg, L2_gnn_w_ih, L2_gnn_b_ih, L2_gnn_w_hh, L2_gnn_b_hh, L3_gnn_W_q, L3_gnn_W_k, L3_gnn_W_v, L3_gnn_W_e, L3_gnn_W_o):
    import jax
    import jax.numpy as jnp

    def _L0_gnn_ref(x, adj, W_t, b_t, W_h, theta):
        import jax, jax.numpy as jnp
        import numpy as np
        B, N, D = (4, 2048, 128)
        DENSITY = 0.02
        in_degrees = jnp.sum(adj, axis=-1)
        norm = jnp.power(in_degrees + 1e-06, -0.5)[..., None]
        f_hom = jnp.einsum('bnd,de->bne', x, theta) * norm
        f_hom = jnp.einsum('bnm,bmd->bnd', adj, f_hom) * norm
        f_het = jnp.einsum('bnd,de->bne', x, W_h)
        gate = jax.nn.sigmoid(jnp.einsum('bnd,de->bne', x, W_t) + b_t)
        out = gate * f_hom + (1.0 - gate) * f_het
        return jax.nn.elu(out)

    def _L1_gnn_ref(x, adj, eps, W1, b1, W2, b2):
        import jax, jax.numpy as jnp
        import numpy as np
        D_IN = 128
        D_HID = 256
        aggregated = jnp.einsum('bnm,bmd->bnd', adj, x)
        h = (1.0 + eps) * x + aggregated
        h = jax.nn.relu(h @ W1 + b1)
        return h @ W2 + b2

    def _L2_gnn_ref(x, mask, w_se, b_se, conv1_w, bn1_g, bn1_b, bn1_m, bn1_v, conv2_w, bn2_g, bn2_b, bn2_m, bn2_v, w_msg, b_msg, w_ih, b_ih, w_hh, b_hh):
        import jax, jax.numpy as jnp
        import numpy as np
        from jax import lax
        DIM = 128
        EPS = 1e-05

        def _bn(h, g, b, m, v):
            scale = g / jnp.sqrt(v + EPS)
            return h * scale[None, :, None] + (b - m * scale)[None, :, None]

        def _conv1d(h, w, pad):
            return lax.conv_general_dilated(h, w, window_strides=(1,), padding=[(pad, pad)], dimension_numbers=('NCH', 'OIH', 'NCH'))
        d = x.shape[-1]
        xc = jnp.transpose(x, (0, 2, 1))
        h = _bn(_conv1d(xc, conv1_w, 0), bn1_g, bn1_b, bn1_m, bn1_v)
        h = jax.nn.relu(h)
        h = _bn(_conv1d(h, conv2_w, 8), bn2_g, bn2_b, bn2_m, bn2_v)
        x_conv = jnp.transpose(jax.nn.relu(h + xc), (0, 2, 1))
        s = x @ w_se.T + b_se
        sq = jnp.sum(s * s, axis=-1)
        dist = sq[:, :, None] + sq[:, None, :] - 2.0 * jnp.einsum('bnd,bmd->bnm', s, s)
        A = jnp.exp(-dist) * mask
        msg = jax.nn.relu(x @ w_msg.T + b_msg)
        x_nmp = jnp.einsum('bnm,bmd->bnd', A, msg)
        x_in = jnp.concatenate([x_conv, x_nmp], axis=-1)
        gi = x_in @ w_ih.T + b_ih
        gh = x @ w_hh.T + b_hh
        gi_r, gi_z, gi_n = (gi[..., :d], gi[..., d:2 * d], gi[..., 2 * d:])
        gh_r, gh_z, gh_n = (gh[..., :d], gh[..., d:2 * d], gh[..., 2 * d:])
        r = jax.nn.sigmoid(gi_r + gh_r)
        z = jax.nn.sigmoid(gi_z + gh_z)
        nn_ = jnp.tanh(gi_n + r * gh_n)
        return (1.0 - z) * nn_ + z * x

    def _L3_gnn_ref(h, edge, adj_mask, W_q, W_k, W_v, W_e, W_o):
        import math
        import jax, jax.numpy as jnp
        import numpy as np
        B, N, D, H = (32, 256, 128, 8)
        HD = D // H
        b, n, _ = h.shape
        q = (h @ W_q.T).reshape(b, n, H, HD).transpose(0, 2, 1, 3)
        k = (h @ W_k.T).reshape(b, n, H, HD).transpose(0, 2, 1, 3)
        v = (h @ W_v.T).reshape(b, n, H, HD).transpose(0, 2, 1, 3)
        edge_bias = jnp.einsum('bij,h->bhij', edge, W_e[:, 0])
        scores = jnp.einsum('bhid,bhjd->bhij', q, k) / math.sqrt(HD) + edge_bias
        scores = jnp.where(adj_mask[:, None], scores, -jnp.inf)
        attn = jax.nn.softmax(scores, axis=-1)
        out = jnp.einsum('bhij,bhjd->bhid', attn, v)
        out = out.transpose(0, 2, 1, 3).reshape(b, n, D)
        return out @ W_o.T
    x = _layernorm(x + _L0_gnn_ref(x, adj, L0_gnn_W_t, L0_gnn_b_t, L0_gnn_W_h, L0_gnn_theta), axis=-1)
    x = _layernorm(x + _L1_gnn_ref(x, adj, L1_gnn_eps, L1_gnn_W1, L1_gnn_b1, L1_gnn_W2, L1_gnn_b2), axis=-1)
    x = _layernorm(x + _L2_gnn_ref(x, adj, L2_gnn_w_se, L2_gnn_b_se, L2_gnn_conv1_w, L2_gnn_bn1_g, L2_gnn_bn1_b, L2_gnn_bn1_m, L2_gnn_bn1_v, L2_gnn_conv2_w, L2_gnn_bn2_g, L2_gnn_bn2_b, L2_gnn_bn2_m, L2_gnn_bn2_v, L2_gnn_w_msg, L2_gnn_b_msg, L2_gnn_w_ih, L2_gnn_b_ih, L2_gnn_w_hh, L2_gnn_b_hh), axis=-1)
    x = _layernorm(x + _L3_gnn_ref(x, adj, adj, L3_gnn_W_q, L3_gnn_W_k, L3_gnn_W_v, L3_gnn_W_e, L3_gnn_W_o), axis=-1)
    return x

_drawn_inputs = setup_inputs


def setup_inputs(seed=0):
    import zlib

    import numpy as np

    out = dict(_drawn_inputs(seed))
    spreads = {'L2_gnn_b_se': (0.0, 2.0),
     'L2_gnn_bn1_g': (1.0, 0.6),
     'L2_gnn_bn1_b': (0.0, 0.391),
     'L2_gnn_bn1_m': (0.0, 0.357),
     'L2_gnn_bn1_v': (1.0, 0.6),
     'L2_gnn_bn2_g': (1.0, 0.562),
     'L2_gnn_bn2_b': (0.0, 0.599),
     'L2_gnn_bn2_m': (0.0, 0.634),
     'L2_gnn_bn2_v': (1.0, 0.6),
     'L2_gnn_b_msg': (0.0, 0.482),
     'L2_gnn_b_ih': (0.0, 0.1),
     'L2_gnn_b_hh': (0.0, 0.372)}
    factors = {'L0_gnn_W_t': 3.929, 'L0_gnn_b_t': 48.502}
    for name, (base, spread) in spreads.items():
        noise = np.random.default_rng([zlib.crc32(name.encode()), seed]).standard_normal(out[name].shape)
        drawn = base * np.exp(spread * noise) if base else spread * noise
        out[name] = jnp.asarray(drawn.astype(out[name].dtype))
    for name, factor in factors.items():
        out[name] = (out[name] * factor).astype(out[name].dtype)
    return out
```

```python
from contextlib import ExitStack

import concourse.bass as bass
from concourse import mybir

F32 = mybir.dt.float32
F32R = mybir.dt.float32r
BF16 = mybir.dt.bfloat16
ALU = mybir.AluOpType
ACT = mybir.ActivationFunctionType
AX_X = mybir.AxisListType.X

P = 128
BATCH = 32
N = 256
D = 128
T = N // P
HEADS = 8
HD = D // HEADS
GH = 4
TAPS = 17
PAD = TAPS // 2
HALF = 64
EPS = 1e-5
MASKED = -1e9

PARTS = [
    ("w0", 3 * D), ("w1", 2 * D), ("w2", 2 * D), ("conv1", D), ("wmsg", D), ("wih", 6 * D), ("whh", 3 * D),
    ("wq", 2 * P), ("wk", 2 * P), ("wv", D), ("wo", D), ("wse", P), ("bt_row", D), ("b2_row", D), ("bmsg_row", D),
    ("we", HEADS), ("ident", P), ("head_rows", GH), ("shift_rows", HEADS), ("eps", 1), ("b1", 2),
    ("bn1", 4), ("bn2", 4), ("bih", 3), ("bhh", 3), ("bse", 1),
]
START, WIDTH, TOTAL = {}, {}, 0
for _name, _width in PARTS:
    START[_name], WIDTH[_name] = TOTAL, _width
    TOTAL += _width


def gnn_stack_kernel(nc, x, xT, adj, adjT, packed, conv2, out):
    ctx = ExitStack()
    with ctx:
        def sb(name, shape, dt=F32):
            return ctx.enter_context(nc.sbuf_tensor(name, shape, dt))

        def sem(name):
            return ctx.enter_context(nc.semaphore(name))

        consts = sb("consts", [P, TOTAL])

        def const(name, lo=0, width=None):
            start = START[name] + lo
            return consts[:, start:start + (WIDTH[name] - lo if width is None else width)]

        conv2_w = sb("conv2_w", [P, TAPS * D])
        conv2_hi = sb("conv2_hi", [P, TAPS * D], F32R)
        conv2_lo = sb("conv2_lo", [P, TAPS * D], F32R)
        ident16 = sb("ident16", [P, P], BF16)
        we_ident = sb("we_ident", [P, HEADS, P], F32R)
        bn_rstd = sb("bn_rstd", [P, 2])
        bn_scale = sb("bn_scale", [P, 2])
        bn_mean = sb("bn_mean", [P, 2])
        bn_bias = sb("bn_bias", [P, 2])
        gate_sum = sb("gate_sum", [P, 2])
        gate_bias = sb("gate_bias", [P, 2])
        one_eps = sb("one_eps", [P, 1])
        minus_half = sb("minus_half", [P, 2])

        x_in = sb("x_in", [P, 2, T, D])
        xT_in = sb("xT_in", [P, 2, N])
        adj_in = sb("adj_in", [P, 2, T, N])
        adjT_in = sb("adjT_in", [P, 2, T, N])
        adj_round = sb("adj_round", [P, 2, T * N], F32R)
        mask = sb("mask", [P, 2, T * N], BF16)
        maskT = sb("maskT", [P, 2, T * N], BF16)

        deg = sb("deg", [P, T])
        deg_eps = sb("deg_eps", [P, T])
        norm = sb("norm", [P, T])
        x_less1 = sb("x_less1", [P, T, D])
        hom_in = sb("hom_in", [P, T, D])
        het = sb("het", [P, T, D])
        gate_pre = sb("gate_pre", [P, T, D])
        gate_tanh = sb("gate_tanh", [P, T, D])
        hom_het = sb("hom_het", [P, T, D])
        gated = sb("gated", [P, T, D])
        mixed = sb("mixed", [P, T, D])
        mixed_exp = sb("mixed_exp", [P, T, D])
        relu_part = sb("relu_part", [P, T, D])
        y = [sb(f"y{k}", [P, T, D]) for k in range(4)]
        stats = [sb(f"stats{k}", [P, T, 6]) for k in range(4)]
        moments = [sb(f"moments{k}", [P, T, 2]) for k in range(4)]
        var_eps = [sb(f"var_eps{k}", [P, T]) for k in range(4)]
        rstd = [sb(f"rstd{k}", [P, T]) for k in range(4)]
        x1 = sb("x1", [P, T, D])
        x1T = sb("x1T", [P, N])
        x1_b2 = sb("x1_b2", [P, T, D])
        hT = sb("hT", [P, N])
        hidT = sb("hidT", [P, 2, N])
        x2 = sb("x2", [P, T, D])
        x2T = sb("x2T", [P, N])
        c1 = sb("c1", [P, N])
        c1_hi = sb("c1_hi", [P, N + 2 * PAD], F32R)
        c1_lo = sb("c1_lo", [P, N + 2 * PAD], F32R)
        dist_l = sb("dist_l", [P, N])
        dist_r = sb("dist_r", [P, N])
        msg_pre = sb("msg_pre", [P, T, D])
        msg = sb("msg", [P, T, D])
        near = sb("near", [P, T * N])
        nearT = sb("nearT", [P, T * N])
        conv_sum = sb("conv_sum", [P, N])
        convT = sb("convT", [P, N])
        nmpT = sb("nmpT", [P, N])
        r_tanh = sb("r_tanh", [P, N])
        z_tanh = sb("z_tanh", [P, N])
        hn_half = sb("hn_half", [P, N])
        r_hn = sb("r_hn", [P, N])
        n_pre = sb("n_pre", [P, N])
        nT = sb("nT", [P, N])
        x_less_n = sb("x_less_n", [P, N])
        z_part = sb("z_part", [P, N])
        n_plus_x = sb("n_plus_x", [P, N])
        y2T = sb("y2T", [P, N])
        x3 = sb("x3", [P, T, D])
        x3T = sb("x3T", [P, N])
        q_hilo = sb("q_hilo", [P, 2, N], F32R)
        q_shift = sb("q_shift", [P, 2, N], F32R)
        k_hi = sb("k_hi", [P, 2, N], F32R)
        k_lo = sb("k_lo", [P, 2, N], F32R)
        kh_head = sb("kh_head", [P, HEADS, N], F32R)
        kl_head = sb("kl_head", [P, HEADS, N], F32R)
        v_one = sb("v_one", [P, T, HEADS, 32])
        maxima = sb("maxima", [P, T, P])
        weights = sb("weights", [P, 3, T * N])
        oT = sb("oT", [P, 2, N])
        inv_sum = sb("inv_sum", [P, T * HEADS])
        o = sb("o", [P, T, D])
        oT_all = sb("oT_all", [P, N])
        result = sb("result", [P, T, D])

        la, lb, lc = (ctx.enter_context(nc.psum_tensor(f"layer_bank{i}", [P, 512], F32)) for i in range(3))
        score = ctx.enter_context(nc.psum_tensor("score_banks", [P, 4, 512], F32))
        att = ctx.enter_context(nc.psum_tensor("att_bank", [P, 512], F32))

        products = """
            const_loaded conv2_loaded setup_dve setup_pool setup_chain pool_chain pool_passed sp_passed dve_passed
            loaded stored
            deg deg_eps norm x_less1 proj0 hom_in gate_pre het gate_tanh agg0 hom_het gated mixed mixed_exp relu_part
            x1 x1_pT x1T agg1 hT hid_p hidT out1_p x1_b2
            x2 x2_pT x2T conv1_p c1_hi c1 c1_lo se_p dist_dve dist_act msg_p msg_pre msg dist_p near nearT
            conv2_p conv_sum convT nmp_p nmpT rz_p r_tanh z_tanh gn_p hn_half r_hn n_pre nT x_less_n z_part n_plus_x
            y2T y2_p x3 x3_pT x3T
            q_p q_hi q_lo q_copy k_p k_hi k_lo kh_head kl_head v_p v_one masks s1_p maxima max_pT shift
            s2_p biased weight pv oT o_p inv_sum o o_pT oT_all wo_p result
        """.split()
        ready = {name: sem(f"{name}_ready") for name in products}
        y_ready = [sem(f"y{k}_ready") for k in range(4)]
        stats_ready = [sem(f"stats{k}_ready") for k in range(4)]
        moments_ready = [sem(f"moments{k}_ready") for k in range(4)]
        var_eps_ready = [sem(f"var_eps{k}_ready") for k in range(4)]
        rstd_ready = [sem(f"rstd{k}_ready") for k in range(4)]
        block = ctx.enter_context(nc.Block())

        def wait(eng, semaphore, count):
            if not isinstance(count, int) or count > 0:
                eng.wait_ge(semaphore, count)

        def count(eng, value):
            return value if isinstance(value, int) else eng.snap(value)

        def steps(eng, body):
            body(0, 0, True, False)
            with eng.Fori(0, BATCH // 2 - 1) as i:
                for half in (0, 1):
                    body(i * 2 + (1 + half), 1 - half, True, True)
            body(BATCH - 1, 1, True, True)
            body(BATCH, 0, False, True)

        @block.sync
        def _(sp):
            def load(graph, buf):
                at = bass.ds(graph, 1)
                sp.dma_start(x_in[:, buf], x[at].rearrange("o (t p) d -> p (o t) d", p=P)).then_inc(ready["loaded"], 16)
                sp.dma_start(xT_in[:, buf], xT[at].rearrange("o d n -> d (o n)")).then_inc(ready["loaded"], 16)
                sp.dma_start(adj_in[:, buf], adj[at].rearrange("o (t p) m -> p (o t) m", p=P)).then_inc(ready["loaded"], 16)
                sp.dma_start(adjT_in[:, buf], adjT[at].rearrange("o (t p) n -> p (o t) n", p=P)).then_inc(ready["loaded"], 16)

            def next_load(s, buf):
                loads, heads = count(sp, s * 64 + 64), count(sp, s * HEADS)
                sp.wait_ge(ready["loaded"], loads)
                sp.nop().then_inc(ready["sp_passed"], 1)
                sp.wait_ge(ready["biased"], heads)
                sp.nop().then_inc(ready["sp_passed"], 1)
                load(s + 1, buf)

            sp.nop().then_inc(ready["stored"], 16)
            sp.dma_start(consts[:], packed).then_inc(ready["const_loaded"], 16)
            load(0, 0)
            sp.dma_start(conv2_w[:], conv2).then_inc(ready["conv2_loaded"], 16)
            sp.wait_ge(ready["loaded"], 64)
            load(1, 1)
            with sp.Fori(0, BATCH // 2 - 1) as i:
                for half in (0, 1):
                    next_load(i * 2 + (1 + half), half)
            sp.wait_ge(ready["stored"], 16 * (BATCH + 1))

        @block.gpsimd
        def _(pool):
            links = [0]

            def link(instruction):
                links[0] += 1
                instruction.then_inc(ready["pool_chain"], 1)
                pool.wait_ge(ready["pool_chain"], links[0])

            link(pool.memset(minus_half[:], -0.5))
            pool.wait_ge(ready["const_loaded"], 16)
            for k, bn in enumerate(("bn1", "bn2")):
                link(pool.tensor_scalar(bn_mean[:, k:k + 1], const(bn, 3, 1), EPS, None, ALU.add))
                pool.tensor_tensor(bn_rstd[:, k:k + 1], bn_mean[:, k:k + 1], minus_half[:, 0:1], ALU.pow).then_inc(ready["setup_pool"], 1)

            def layer_norm(k, n, n2):
                pool.wait_ge(moments_ready[k], n2)
                pool.nop().then_inc(ready["pool_passed"], 1)
                pool.tensor_scalar(var_eps[k][:], moments[k][:, :, 1], EPS, None, ALU.add).then_inc(var_eps_ready[k], 1)
                pool.wait_ge(var_eps_ready[k], n)
                pool.tensor_tensor(rstd[k][:], var_eps[k][:], minus_half[:], ALU.pow).then_inc(rstd_ready[k], 1)

            def body(s, buf, layers, attention):
                n, m = count(pool, s + 1), count(pool, s)
                n2, m2, n64 = count(pool, (s + 1) * 2), count(pool, s * 2), count(pool, (s + 1) * 64)
                if layers:
                    pool.wait_ge(ready["deg"], n)
                    pool.nop().then_inc(ready["pool_passed"], 1)
                    pool.tensor_scalar(deg_eps[:], deg[:], 1e-6, None, ALU.add).then_inc(ready["deg_eps"], 1)
                    pool.wait_ge(ready["deg_eps"], n)
                    pool.tensor_tensor(norm[:], deg_eps[:], minus_half[:], ALU.pow).then_inc(ready["norm"], 1)
                    pool.wait_ge(ready["loaded"], n64)
                    pool.nop().then_inc(ready["pool_passed"], 1)
                    wait(pool, ready["relu_part"], m)
                    pool.nop().then_inc(ready["pool_passed"], 1)
                    pool.tensor_scalar(x_less1[:], x_in[:, buf], -1.0, None, ALU.add).then_inc(ready["x_less1"], 1)
                if attention:
                    pool.wait_ge(ready["k_hi"], m)
                    pool.nop().then_inc(ready["pool_passed"], 1)
                    for h in range(HEADS):
                        pool.tensor_scalar(kh_head[:, h], k_hi[:, h // GH].bitcast(F32), const("head_rows", h % GH, 1), None,
                                           ALU.mult).then_inc(ready["kh_head"], 1)
                    pool.wait_ge(ready["q_hi"], m)
                    pool.nop().then_inc(ready["pool_passed"], 1)
                    pool.tensor_scalar(q_shift[0:HALF], q_hilo[0:HALF].bitcast(F32), 1.0, None, ALU.mult).then_inc(ready["q_copy"], 1)
                if layers:
                    layer_norm(0, n, n2)
                    pool.wait_ge(ready["x1"], n2)
                    pool.tensor_tensor(x1_b2[:], x1[:], const("b2_row").rearrange("p (o d) -> p o d", o=1).broadcast_to([P, T, D]),
                                       ALU.add).then_inc(ready["x1_b2"], 1)
                if attention:
                    pool.wait_ge(ready["k_lo"], m)
                    pool.nop().then_inc(ready["pool_passed"], 1)
                    for h in range(HEADS):
                        pool.tensor_scalar(kl_head[0:HALF, h], k_lo[0:HALF, h // GH].bitcast(F32),
                                           const("head_rows", h % GH, 1)[0:HALF], None, ALU.mult).then_inc(ready["kl_head"], 1)
                if layers:
                    layer_norm(1, n, n2)
                    pool.tensor_scalar(mask[:, buf], adj_in[:, buf].rearrange("p t m -> p (t m)"), 0.0, MASKED,
                                       ALU.is_equal, ALU.mult).then_inc(ready["masks"], 1)
                    pool.tensor_scalar(maskT[:, buf], adjT_in[:, buf].rearrange("p t m -> p (t m)"), 0.0, MASKED,
                                       ALU.is_equal, ALU.mult).then_inc(ready["masks"], 1)
                    pool.tensor_scalar(adj_round[:, buf], adj_in[:, buf].rearrange("p t m -> p (t m)"), 1.0, None,
                                       ALU.mult).then_inc(ready["masks"], 1)
                    pool.wait_ge(ready["msg_pre"], n)
                    pool.nop().then_inc(ready["pool_passed"], 1)
                    pool.tensor_scalar(msg[:], msg_pre[:], 0.0, None, ALU.max).then_inc(ready["msg"], 1)
                if attention:
                    layer_norm(3, m, m2)
                if layers:
                    pool.wait_ge(ready["nT"], n)
                    pool.tensor_tensor(n_plus_x[:], nT[:], x2T[:], ALU.add).then_inc(ready["n_plus_x"], 1)
                    layer_norm(2, n, n2)

            steps(pool, body)

        @block.scalar
        def _(act):
            act.wait_ge(ready["setup_dve"], 1)

            def body(s, buf, layers, attention):
                n, m = count(act, s + 1), count(act, s)

                def exponentials(h):
                    act.wait_ge(ready["biased"], s * HEADS - (HEADS - 1 - h))
                    act.activation(weights[:, h % 3], weights[:, h % 3], ACT.Exp).then_inc(ready["weight"], 1)

                if layers:
                    act.wait_ge(ready["proj0"], n)
                    act.wait_ge(ready["norm"], n)
                    for t in range(T):
                        act.activation(hom_in[:, t], (la, lb)[t][:, 0:D], ACT.Copy, scale=norm[:, t:t + 1]).then_inc(ready["hom_in"], 1)
                if attention:
                    act.wait_ge(ready["q_p"], m)
                    act.activation(q_hilo[:], score[:, 0].rearrange("p (g n) -> p g n", g=2), ACT.Copy, scale=HD ** -0.5).then_inc(ready["q_hi"], 1)
                    act.wait_ge(ready["k_p"], m)
                    act.activation(k_hi[:], score[:, 1].rearrange("p (g n) -> p g n", g=2), ACT.Copy).then_inc(ready["k_hi"], 1)
                    act.wait_ge(ready["v_p"], m)
                    act.activation(v_one[:, :, :, 0:HD], att[:, 0:N].rearrange("p (t h d) -> p t h d", t=T, h=HEADS), ACT.Copy).then_inc(ready["v_one"], 1)
                if layers:
                    act.wait_ge(ready["gate_pre"], n)
                    act.activation(gate_tanh[:], gate_pre[:], ACT.Tanh, scale=0.5).then_inc(ready["gate_tanh"], 1)
                    act.wait_ge(ready["mixed"], n)
                    act.activation(mixed_exp[:], mixed[:], ACT.Exp).then_inc(ready["mixed_exp"], 1)
                    act.wait_ge(ready["x1_pT"], n)
                    act.activation(x1T[:], la[:, 0:N], ACT.Copy).then_inc(ready["x1T"], 1)
                if attention:
                    act.wait_ge(ready["max_pT"], m)
                    for g in range(2):
                        act.activation(q_shift[HALF:HALF + 32, g], att[HALF:HALF + 32, 0:N], ACT.Copy, scale=-1.0).then_inc(ready["shift"], 1)
                    exponentials(0)
                if layers:
                    act.wait_ge(ready["hid_p"], n)
                    for k in range(2):
                        act.activation(hidT[:, k], lc[:, k * N:(k + 1) * N], ACT.Relu, bias=const("b1", k, 1)).then_inc(ready["hidT"], 1)
                if attention:
                    exponentials(1)
                    exponentials(2)
                    exponentials(3)
                if layers:
                    act.wait_ge(ready["x2_pT"], n)
                    act.activation(x2T[:], la[:, 0:N], ACT.Copy).then_inc(ready["x2T"], 1)
                if attention:
                    exponentials(4)
                if layers:
                    act.wait_ge(ready["conv1_p"], n)
                    for dst, name in ((c1_hi[:, PAD:PAD + N], "c1_hi"), (c1[:], "c1")):
                        act.activation(dst, lb[:, 0:N], ACT.Relu, bias=bn_bias[:, 0:1], scale=bn_scale[:, 0:1]).then_inc(ready[name], 1)
                    act.wait_ge(ready["se_p"], n)
                    act.activation(dist_r[32:64], lc[32:64, 0:N], ACT.Square, bias=const("bse")[32:64]).then_inc(ready["dist_act"], 1)
                    act.activation(dist_l[64:96], lc[64:96, 0:N], ACT.Square, bias=const("bse")[64:96]).then_inc(ready["dist_act"], 1)
                if attention:
                    exponentials(5)
                if layers:
                    act.wait_ge(ready["dist_p"], n)
                    act.activation(near[:], lc[:], ACT.Exp, scale=2.0).then_inc(ready["near"], 1)
                if attention:
                    exponentials(6)
                    exponentials(7)
                    act.wait_ge(ready["pv"], s * HEADS)
                    act.activation(oT[:], att[:].rearrange("p (g n) -> p g n", g=2), ACT.Copy).then_inc(ready["oT"], 1)
                if layers:
                    act.wait_ge(ready["nmp_p"], n)
                    act.activation(nmpT[:], la[:, 0:N], ACT.Copy).then_inc(ready["nmpT"], 1)
                    act.wait_ge(ready["conv_sum"], n)
                    act.activation(convT[:], conv_sum[:], ACT.Relu, bias=bn_bias[:, 1:2]).then_inc(ready["convT"], 1)
                if attention:
                    act.wait_ge(ready["o_pT"], m)
                    act.activation(oT_all[:], score[:, 1, 0:N], ACT.Copy).then_inc(ready["oT_all"], 1)
                if layers:
                    act.wait_ge(ready["rz_p"], n)
                    act.activation(r_tanh[:], lc[:, 0:N], ACT.Tanh, bias=gate_bias[:, 0:1], scale=0.5).then_inc(ready["r_tanh"], 1)
                    act.activation(z_tanh[:], lc[:, N:2 * N], ACT.Tanh, bias=gate_bias[:, 1:2], scale=0.5).then_inc(ready["z_tanh"], 1)
                    act.wait_ge(ready["n_pre"], n)
                    act.activation(nT[:], n_pre[:], ACT.Tanh, bias=const("bih", 2, 1)).then_inc(ready["nT"], 1)
                if attention:
                    act.wait_ge(ready["result"], s * 2)
                    act.dma_start(out[bass.ds(s - 1, 1)].rearrange("o (t p) d -> p (o t) d", p=P), result[:]).then_inc(ready["stored"], 16)
                if layers:
                    act.wait_ge(ready["x3_pT"], n)
                    act.activation(x3T[:], lc[:, 0:N], ACT.Copy).then_inc(ready["x3T"], 1)

            steps(act, body)

        @block.vector
        def _(dve):
            links = [0]

            def link(instruction):
                links[0] += 1
                instruction.then_inc(ready["setup_chain"], 1)
                dve.wait_ge(ready["setup_chain"], links[0])

            link(dve.memset(c1_hi[:].bitcast(F32), 0.0))
            link(dve.memset(c1_lo[:].bitcast(F32), 0.0))
            link(dve.memset(maxima[:], 0.0))
            link(dve.memset(q_shift[:].bitcast(F32), 0.0))
            link(dve.memset(kl_head[:].bitcast(F32), 0.0))
            link(dve.memset(v_one[:], 0.0))
            link(dve.memset(v_one[:, :, :, HD:HD + 1], 1.0))
            link(dve.memset(dist_l[32:64], -0.5))
            link(dve.memset(dist_r[64:96], -0.5))
            dve.wait_ge(ready["const_loaded"], 16)
            link(dve.tensor_copy(ident16[:], const("ident")))
            for h in range(HEADS):
                link(dve.tensor_scalar(we_ident[:, h], const("ident"), const("we", h, 1), None, ALU.mult))
                link(dve.tensor_scalar(kl_head[HALF:P, h], kl_head[HALF:P, h].bitcast(F32), const("shift_rows", h, 1)[HALF:P], None, ALU.add))
            dve.wait_ge(ready["setup_pool"], 2)
            for k, bn in enumerate(("bn1", "bn2")):
                link(dve.tensor_tensor(bn_scale[:, k:k + 1], bn_rstd[:, k:k + 1], const(bn, 0, 1), ALU.mult))
                link(dve.tensor_tensor(bn_mean[:, k:k + 1], const(bn, 2, 1), bn_scale[:, k:k + 1], ALU.mult))
                link(dve.tensor_tensor(bn_bias[:, k:k + 1], const(bn, 1, 1), bn_mean[:, k:k + 1], ALU.subtract))
            link(dve.tensor_tensor(gate_sum[:], const("bih", 0, 2), const("bhh", 0, 2), ALU.add))
            link(dve.tensor_scalar(gate_bias[:], gate_sum[:], 0.5, None, ALU.mult))
            link(dve.tensor_scalar(one_eps[:], const("eps"), 1.0, None, ALU.add))
            dve.wait_ge(ready["conv2_loaded"], 16)
            link(dve.tensor_copy(conv2_hi[:], conv2_w[:]))
            link(dve.tensor_tensor(conv2_lo[:], conv2_w[:], conv2_hi[:].bitcast(F32), ALU.subtract))
            dve.nop().then_inc(y_ready[3], 1)
            dve.nop().then_inc(ready["setup_dve"], 1)

            def moments_of(k, n2, src):
                for t in range(T):
                    dve.bn_stats(stats[k][:, t], src(t)).then_inc(stats_ready[k], 1)
                dve.wait_ge(stats_ready[k], n2)
                dve.nop().then_inc(ready["dve_passed"], 1)
                for t in range(T):
                    dve.bn_aggr(moments[k][:, t], stats[k][:, t]).then_inc(moments_ready[k], 1)

            def normalise(k, n, n2, dst, src, name):
                dve.wait_ge(moments_ready[k], n2)
                dve.wait_ge(rstd_ready[k], n)
                for t in range(T):
                    dve.tensor_scalar(dst[:, t], src(t), moments[k][:, t, 0:1], rstd[k][:, t:t + 1],
                                      ALU.subtract, ALU.mult).then_inc(ready[name], 1)

            def body(s, buf, layers, attention):
                n, m, n2, m2 = count(dve, s + 1), count(dve, s), count(dve, s * 2 + 2), count(dve, s * 2)
                heads = [s * HEADS - (HEADS - 1 - h) for h in range(HEADS)]

                def maximum(pair):
                    dve.wait_ge(ready["s1_p"], s * 4 - (3 - pair))
                    banks = score[:, 2 * (pair % 2):2 * (pair % 2) + 2].rearrange("p h (t j) -> p h t j", t=T)
                    dst = maxima[:, :, HALF + 2 * pair:HALF + 2 * pair + 2].rearrange("p t h -> p h t")
                    dve.tensor_reduce(dst, banks, AX_X, ALU.max).then_inc(ready["maxima"], 1)

                def bias(h):
                    dve.wait_ge(ready["s2_p"], heads[h])
                    if h >= 3:
                        dve.wait_ge(ready["pv"], heads[h - 3])
                    dve.scalar_tensor_tensor(out=weights[:, h % 3], in0=adjT_in[:, 1 - buf].rearrange("p t n -> p (t n)"),
                                             scalar=const("we", h, 1), in1=score[:, h % 4], op0=ALU.mult, op1=ALU.add
                                             ).then_inc(ready["biased"], 1)

                if layers:
                    dve.wait_ge(ready["loaded"], n * 64)
                    dve.tensor_reduce(deg[:], adj_in[:, buf], AX_X, ALU.add).then_inc(ready["deg"], 1)
                    dve.wait_ge(ready["hom_in"], n2)
                    for t in range(T):
                        dve.tensor_tensor(gate_pre[:, t], (la, lb)[t][:, 2 * D:3 * D], const("bt_row"), ALU.add)
                        last = dve.tensor_copy(het[:, t], (la, lb)[t][:, D:2 * D])
                    last.then_inc(ready["het"], 1)
                    dve.wait_ge(ready["het"], n)
                    dve.nop().then_inc(ready["gate_pre"], 1)
                if attention:
                    dve.wait_ge(ready["q_hi"], m)
                    dve.scalar_tensor_tensor(out=q_hilo[HALF:P], in0=score[HALF:P, 0].rearrange("p (g n) -> p g n", g=2), scalar=HD ** -0.5,
                                             in1=q_hilo[HALF:P].bitcast(F32), op0=ALU.mult, op1=ALU.subtract).then_inc(ready["q_lo"], 1)
                    dve.wait_ge(ready["k_hi"], m)
                    dve.tensor_tensor(k_lo[0:HALF], score[0:HALF, 1].rearrange("p (g n) -> p g n", g=2), k_hi[0:HALF].bitcast(F32),
                                      ALU.subtract).then_inc(ready["k_lo"], 1)
                    maximum(0)
                if layers:
                    dve.wait_ge(ready["agg0"], n)
                    for t in range(T):
                        dve.scalar_tensor_tensor(out=hom_het[:, t], in0=lc[:, t * D:(t + 1) * D], scalar=norm[:, t:t + 1], in1=het[:, t],
                                                 op0=ALU.mult, op1=ALU.subtract).then_inc(ready["hom_het"], 1)
                    dve.wait_ge(ready["hom_het"], n2)
                    dve.wait_ge(ready["gate_tanh"], n)
                    dve.scalar_tensor_tensor(out=gated[:], in0=gate_tanh[:], scalar=1.0, in1=hom_het[:], op0=ALU.add,
                                             op1=ALU.mult).then_inc(ready["gated"], 1)
                    dve.wait_ge(ready["gated"], n)
                    dve.scalar_tensor_tensor(out=mixed[:], in0=gated[:], scalar=0.5, in1=het[:], op0=ALU.mult,
                                             op1=ALU.add).then_inc(ready["mixed"], 1)
                if attention:
                    maximum(1)
                if layers:
                    dve.wait_ge(ready["mixed"], n)
                    dve.wait_ge(ready["x_less1"], n)
                    dve.scalar_tensor_tensor(out=relu_part[:], in0=mixed[:], scalar=0.0, in1=x_less1[:], op0=ALU.max,
                                             op1=ALU.add).then_inc(ready["relu_part"], 1)
                    dve.wait_ge(ready["relu_part"], n)
                    dve.wait_ge(ready["mixed_exp"], n)
                    dve.scalar_tensor_tensor(out=y[0][:], in0=mixed_exp[:], scalar=1.0, in1=relu_part[:], op0=ALU.min,
                                             op1=ALU.add).then_inc(y_ready[0], 1)
                    dve.wait_ge(y_ready[0], n)
                    moments_of(0, n2, lambda t: y[0][:, t])
                if attention:
                    maximum(2)
                    maximum(3)
                if layers:
                    normalise(0, n, n2, x1, lambda t: y[0][:, t], "x1")
                if attention:
                    bias(0)
                if layers:
                    dve.wait_ge(ready["agg1"], n)
                    dve.wait_ge(ready["x1T"], n)
                    dve.scalar_tensor_tensor(out=hT[:], in0=x1T[:], scalar=one_eps[:], in1=lb[:, 0:N], op0=ALU.mult,
                                             op1=ALU.add).then_inc(ready["hT"], 1)
                if attention:
                    bias(1)
                    bias(2)
                if layers:
                    dve.wait_ge(ready["out1_p"], n)
                    dve.wait_ge(ready["x1_b2"], n)
                    dve.tensor_tensor(y[1][:], lb[:, 0:N].rearrange("p (t d) -> p t d", t=T), x1_b2[:], ALU.add).then_inc(y_ready[1], 1)
                    dve.wait_ge(y_ready[1], n)
                    moments_of(1, n2, lambda t: y[1][:, t])
                if attention:
                    bias(3)
                if layers:
                    normalise(1, n, n2, x2, lambda t: y[1][:, t], "x2")
                if attention:
                    bias(4)
                if layers:
                    dve.wait_ge(ready["se_p"], n)
                    for dst in (dist_l, dist_r):
                        dve.tensor_scalar(dst[0:32], lc[0:32, 0:N], const("bse")[0:32], None, ALU.add).then_inc(ready["dist_dve"], 1)
                    dve.wait_ge(ready["msg_p"], n)
                    dve.tensor_tensor(msg_pre[:], la[:, 0:N].rearrange("p (t d) -> p t d", t=T),
                                      const("bmsg_row").rearrange("p (o d) -> p o d", o=1).broadcast_to([P, T, D]), ALU.add
                                      ).then_inc(ready["msg_pre"], 1)
                    dve.wait_ge(ready["c1"], n)
                    dve.wait_ge(ready["c1_hi"], n)
                    dve.tensor_tensor(c1_lo[:, PAD:PAD + N], c1[:], c1_hi[:, PAD:PAD + N].bitcast(F32), ALU.subtract).then_inc(ready["c1_lo"], 1)
                if attention:
                    bias(5)
                if layers:
                    dve.wait_ge(ready["near"], n)
                    dve.tensor_tensor(nearT[:], near[:], adjT_in[:, buf].rearrange("p t n -> p (t n)"), ALU.mult).then_inc(ready["nearT"], 1)
                if attention:
                    bias(6)
                    bias(7)
                if layers:
                    dve.wait_ge(ready["conv2_p"], n)
                    dve.scalar_tensor_tensor(out=conv_sum[:], in0=lb[:, 0:N], scalar=bn_scale[:, 1:2], in1=x2T[:], op0=ALU.mult,
                                             op1=ALU.add).then_inc(ready["conv_sum"], 1)
                if attention:
                    dve.wait_ge(ready["o_p"], m)
                    by_head = score[:, 0].rearrange("p (a c) -> p a c", c=32)
                    dve.reciprocal(inv_sum[:].rearrange("p (a o) -> p a o", o=1), by_head[:, :, HD:HD + 1]).then_inc(ready["inv_sum"], 1)
                    dve.wait_ge(ready["inv_sum"], m)
                    dve.tensor_tensor(o[:].rearrange("p t (h d) -> p (t h) d", d=HD), by_head[:, :, 0:HD],
                                      inv_sum[:].rearrange("p (a o) -> p a o", o=1).broadcast_to([P, T * HEADS, HD]), ALU.mult
                                      ).then_inc(ready["o"], 1)
                if layers:
                    dve.wait_ge(ready["gn_p"], n)
                    dve.tensor_scalar(hn_half[:], lb[:, N:2 * N], const("bhh", 2, 1), 0.5, ALU.add, ALU.mult).then_inc(ready["hn_half"], 1)
                    dve.wait_ge(ready["hn_half"], n)
                    dve.wait_ge(ready["r_tanh"], n)
                    dve.scalar_tensor_tensor(out=r_hn[:], in0=r_tanh[:], scalar=1.0, in1=hn_half[:], op0=ALU.add,
                                             op1=ALU.mult).then_inc(ready["r_hn"], 1)
                    dve.wait_ge(ready["r_hn"], n)
                    dve.tensor_tensor(n_pre[:], lb[:, 0:N], r_hn[:], ALU.add).then_inc(ready["n_pre"], 1)
                if attention:
                    dve.wait_ge(ready["wo_p"], m)
                    dve.tensor_tensor(y[3][:], score[:, 1, N:2 * N].rearrange("p (t d) -> p t d", t=T), x3[:], ALU.add).then_inc(y_ready[3], 1)
                    dve.wait_ge(y_ready[3], n)
                    moments_of(3, m2, lambda t: y[3][:, t])
                if layers:
                    dve.wait_ge(ready["nT"], n)
                    dve.tensor_tensor(x_less_n[:], x2T[:], nT[:], ALU.subtract).then_inc(ready["x_less_n"], 1)
                    dve.wait_ge(ready["x_less_n"], n)
                    dve.wait_ge(ready["z_tanh"], n)
                    dve.scalar_tensor_tensor(out=z_part[:], in0=z_tanh[:], scalar=1.0, in1=x_less_n[:], op0=ALU.add,
                                             op1=ALU.mult).then_inc(ready["z_part"], 1)
                    dve.wait_ge(ready["z_part"], n)
                    dve.wait_ge(ready["n_plus_x"], n)
                    dve.scalar_tensor_tensor(out=y2T[:], in0=z_part[:], scalar=0.5, in1=n_plus_x[:], op0=ALU.mult,
                                             op1=ALU.add).then_inc(ready["y2T"], 1)
                if attention:
                    dve.wait_ge(ready["stored"], s * 16)
                    normalise(3, m, m2, result, lambda t: y[3][:, t], "result")
                if layers:
                    dve.wait_ge(ready["y2_p"], n)
                    moments_of(2, n2, lambda t: la[:, t * D:(t + 1) * D])
                    normalise(2, n, n2, x3, lambda t: la[:, t * D:(t + 1) * D], "x3")

            steps(dve, body)

        @block.tensor
        def _(pe):
            pe.wait_ge(ready["setup_dve"], 1)

            def turn(dst, src, name):
                for t in range(T):
                    last = pe.transpose(dst[:, t * P:(t + 1) * P], src(t), const("ident"))
                last.then_inc(ready[name], 1)

            def body(s, buf, layers, attention):
                n, m, n2 = count(pe, s + 1), count(pe, s), count(pe, s * 2 + 2)

                def scores_for_maxima(pair):
                    for h in (2 * pair, 2 * pair + 1):
                        bank = score[:, h % 4]
                        pe.matmul(bank, ident16[:], mask[:, 1 - buf], start=True, stop=False)
                        pe.matmul(bank, we_ident[:, h], adj_round[:, 1 - buf], start=False, stop=False)
                        for t in range(T):
                            last = pe.matmul(bank[:, t * N:(t + 1) * N], q_hilo[:, h // GH, t * P:(t + 1) * P], kh_head[:, h],
                                             start=False, stop=t == T - 1)
                    last.then_inc(ready["s1_p"], 1)

                def scores(h):
                    if h >= 4:
                        pe.wait_ge(ready["biased"], s * HEADS - (HEADS + 3 - h))
                    bank = score[:, h % 4]
                    pe.matmul(bank, ident16[:], maskT[:, 1 - buf], start=True, stop=False)
                    for t in range(T):
                        cols = bank[:, t * N:(t + 1) * N]
                        pe.matmul(cols, kh_head[:, h, t * P:(t + 1) * P], q_hilo[:, h // GH], start=False, stop=False)
                        last = pe.matmul(cols, kl_head[:, h, t * P:(t + 1) * P], q_shift[:, h // GH], start=False, stop=t == T - 1)
                    last.then_inc(ready["s2_p"], 1)

                def weigh(h):
                    pe.wait_ge(ready["weight"], s * HEADS - (HEADS - 1 - h))
                    rows = 32 * (h % GH)
                    for t in range(T):
                        last = pe.matmul(att[rows:rows + 32, (h // GH) * N:(h // GH + 1) * N], v_one[:, t, h],
                                         weights[:, h % 3, t * N:(t + 1) * N], start=t == 0, stop=t == T - 1)
                    last.then_inc(ready["pv"], 1)

                if layers:
                    pe.wait_ge(ready["loaded"], s * 64 + 64)
                    wait(pe, ready["x3"], s * 2)
                    for t in range(T):
                        last = pe.matmul((la, lb)[t][:, 0:3 * D], xT_in[:, buf, t * P:(t + 1) * P], const("w0"), start=True, stop=True)
                    last.then_inc(ready["proj0"], 1)
                if attention:
                    pe.wait_ge(ready["x3T"], m)
                    pe.wait_ge(y_ready[3], s)
                    for dst, w, name in ((score[:, 0], "wq", "q_p"), (score[:, 1], "wk", "k_p")):
                        for g in range(2):
                            last = pe.matmul(dst[:, g * N:(g + 1) * N], const(w, g * P, P), x3T[:], start=True, stop=True)
                        last.then_inc(ready[name], 1)
                    for t in range(T):
                        last = pe.matmul(att[:, t * D:(t + 1) * D], x3T[:, t * P:(t + 1) * P], const("wv"), start=True, stop=True)
                    last.then_inc(ready["v_p"], 1)
                    pe.wait_ge(ready["masks"], s * 3)
                    pe.wait_ge(ready["q_lo"], m)
                    pe.wait_ge(ready["k_lo"], m)
                    pe.wait_ge(ready["kh_head"], s * HEADS)
                    scores_for_maxima(0)
                    scores_for_maxima(1)
                if layers:
                    pe.wait_ge(ready["hom_in"], n2)
                    wait(pe, ready["x3T"], s)
                    for t in range(T):
                        for k in range(T):
                            last = pe.matmul(lc[:, t * D:(t + 1) * D], adjT_in[:, buf, k, t * P:(t + 1) * P], hom_in[:, k],
                                             start=k == 0, stop=k == T - 1)
                    last.then_inc(ready["agg0"], 1)
                if attention:
                    for pair in (2, 3):
                        pe.wait_ge(ready["maxima"], s * 4 - (5 - pair))
                        scores_for_maxima(pair)
                    pe.wait_ge(ready["maxima"], s * 4)
                    pe.wait_ge(ready["v_one"], m)
                    turn(att, lambda t: maxima[:, t], "max_pT")
                if layers:
                    pe.wait_ge(ready["x1"], n2)
                    turn(la, lambda t: x1[:, t], "x1_pT")
                    for k in range(T):
                        last = pe.matmul(lb[:, 0:N], x1[:, k], adjT_in[:, buf, k], start=k == 0, stop=k == T - 1)
                    last.then_inc(ready["agg1"], 1)
                if attention:
                    pe.wait_ge(ready["shift"], s * 2)
                    pe.wait_ge(ready["q_copy"], m)
                    pe.wait_ge(ready["kl_head"], s * HEADS)
                    scores(0)
                    scores(1)
                if layers:
                    pe.wait_ge(ready["hT"], n)
                    for k in range(2):
                        last = pe.matmul(lc[:, k * N:(k + 1) * N], const("w1", k * P, P), hT[:], start=True, stop=True)
                    last.then_inc(ready["hid_p"], 1)
                if attention:
                    scores(2)
                    weigh(0)
                if layers:
                    pe.wait_ge(ready["hidT"], n2)
                    for t in range(T):
                        for k in range(2):
                            last = pe.matmul(lb[:, t * D:(t + 1) * D], hidT[:, k, t * P:(t + 1) * P], const("w2", k * D, D),
                                             start=k == 0, stop=k == 1)
                    last.then_inc(ready["out1_p"], 1)
                if attention:
                    scores(3)
                    weigh(1)
                    scores(4)
                    weigh(2)
                if layers:
                    pe.wait_ge(ready["x2"], n2)
                    turn(la, lambda t: x2[:, t], "x2_pT")
                if attention:
                    scores(5)
                    weigh(3)
                if layers:
                    pe.wait_ge(ready["x2T"], n)
                    pe.matmul(lb[:, 0:N], const("conv1"), x2T[:], start=True, stop=True).then_inc(ready["conv1_p"], 1)
                    pe.matmul(lc[:, 0:N], const("wse"), x2T[:], start=True, stop=True).then_inc(ready["se_p"], 1)
                    for t in range(T):
                        last = pe.matmul(la[:, t * D:(t + 1) * D], x2T[:, t * P:(t + 1) * P], const("wmsg"), start=True, stop=True)
                    last.then_inc(ready["msg_p"], 1)
                if attention:
                    scores(6)
                    weigh(4)
                if layers:
                    pe.wait_ge(ready["dist_dve"], n2)
                    pe.wait_ge(ready["dist_act"], n2)
                    for t in range(T):
                        last = pe.matmul(lc[:, t * N:(t + 1) * N], dist_l[0:96, t * P:(t + 1) * P], dist_r[0:96], start=True, stop=True)
                    last.then_inc(ready["dist_p"], 1)
                if attention:
                    scores(7)
                    weigh(5)
                if layers:
                    pe.wait_ge(ready["c1_lo"], n)
                    for k in range(TAPS):
                        for j, (w, c) in enumerate(((conv2_hi, c1_hi), (conv2_hi, c1_lo), (conv2_lo, c1_hi))):
                            last = pe.matmul(lb[:, 0:N], w[:, k * D:(k + 1) * D], c[:, k:k + N],
                                             start=k == 0 and j == 0, stop=k == TAPS - 1 and j == 2)
                    last.then_inc(ready["conv2_p"], 1)
                if attention:
                    weigh(6)
                    weigh(7)
                if layers:
                    pe.wait_ge(ready["msg"], n)
                    pe.wait_ge(ready["nearT"], n)
                    for k in range(T):
                        last = pe.matmul(la[:, 0:N], msg[:, k], nearT[:, k * N:(k + 1) * N], start=k == 0, stop=k == T - 1)
                    last.then_inc(ready["nmp_p"], 1)
                if attention:
                    pe.wait_ge(ready["oT"], m)
                    for t in range(T):
                        for g in range(2):
                            last = pe.transpose(score[:, 0, (2 * t + g) * P:(2 * t + g + 1) * P], oT[:, g, t * P:(t + 1) * P], const("ident"))
                    last.then_inc(ready["o_p"], 1)
                if layers:
                    pe.wait_ge(ready["nmpT"], n)
                    pe.wait_ge(ready["convT"], n)
                    for g in range(2):
                        dst = lc[:, g * N:(g + 1) * N]
                        pe.matmul(dst, const("whh", g * D, D), x2T[:], start=True, stop=False)
                        pe.matmul(dst, const("wih", 3 * D + g * D, D), nmpT[:], start=False, stop=False)
                        last = pe.matmul(dst, const("wih", g * D, D), convT[:], start=False, stop=True)
                    last.then_inc(ready["rz_p"], 1)
                    pe.matmul(lb[:, N:2 * N], const("whh", 2 * D, D), x2T[:], start=True, stop=True)
                    pe.matmul(lb[:, 0:N], const("wih", 5 * D, D), nmpT[:], start=True, stop=False)
                    pe.matmul(lb[:, 0:N], const("wih", 2 * D, D), convT[:], start=False, stop=True).then_inc(ready["gn_p"], 1)
                if attention:
                    pe.wait_ge(ready["o"], m)
                    turn(score[:, 1], lambda t: o[:, t], "o_pT")
                    pe.wait_ge(ready["oT_all"], m)
                    for t in range(T):
                        last = pe.matmul(score[:, 1, N + t * D:N + (t + 1) * D], oT_all[:, t * P:(t + 1) * P], const("wo"), start=True, stop=True)
                    last.then_inc(ready["wo_p"], 1)
                if layers:
                    pe.wait_ge(ready["y2T"], n)
                    turn(la, lambda t: y2T[:, t * P:(t + 1) * P], "y2_p")
                    pe.wait_ge(ready["x3"], n2)
                    turn(lc, lambda t: x3[:, t], "x3_pT")

            steps(pe, body)


def kernel(**inputs):
    import numpy as np
    import concourse.bacc as bacc
    from concourse.bass_utils import run_bass_kernel_spmd

    a = {name: np.asarray(v) for name, v in inputs.items()}

    def column(v, rows=P):
        return np.broadcast_to(v.reshape(1, -1), (rows, v.size))

    def columns(v, k):
        return v.reshape(k, P).T

    w_se, b_se = a["L2_gnn_w_se"], a["L2_gnn_b_se"]
    wse = np.zeros((D, P), w_se.dtype)
    bse = np.zeros((P, 1), b_se.dtype)
    for start in (0, 32, 64):
        wse[:, start:start + 3] = w_se.T
        bse[start:start + 3, 0] = b_se
    head_rows = np.zeros((P, GH), np.float32)
    shift_rows = np.zeros((P, HEADS), np.float32)
    for h in range(GH):
        for start in (0, HALF):
            head_rows[start + h * HD:start + (h + 1) * HD, h] = 1.0
    for h in range(HEADS):
        shift_rows[HALF + h, h] = 1.0
    twice = lambda w: np.concatenate([w[:, :HALF], w[:, :HALF], w[:, HALF:], w[:, HALF:]], 1)
    tiles = lambda w: np.concatenate(np.split(w, w.shape[0] // P, 0), 1)
    parts = {
        "w0": np.concatenate([a["L0_gnn_theta"], a["L0_gnn_W_h"], a["L0_gnn_W_t"]], 1),
        "w1": a["L1_gnn_W1"],
        "w2": tiles(a["L1_gnn_W2"]),
        "conv1": a["L2_gnn_conv1_w"][:, :, 0].T,
        "wmsg": a["L2_gnn_w_msg"].T,
        "wih": tiles(a["L2_gnn_w_ih"].T),
        "whh": a["L2_gnn_w_hh"].T,
        "wq": twice(a["L3_gnn_W_q"].T),
        "wk": twice(a["L3_gnn_W_k"].T),
        "wv": a["L3_gnn_W_v"].T,
        "wo": a["L3_gnn_W_o"].T,
        "wse": wse,
        "bt_row": column(a["L0_gnn_b_t"]),
        "b2_row": column(a["L1_gnn_b2"]),
        "bmsg_row": column(a["L2_gnn_b_msg"]),
        "we": column(a["L3_gnn_W_e"]),
        "ident": np.eye(P, dtype=np.float32),
        "head_rows": head_rows,
        "shift_rows": shift_rows,
        "eps": column(a["L1_gnn_eps"]),
        "b1": columns(a["L1_gnn_b1"], 2),
        "bn1": np.stack([a[f"L2_gnn_bn1_{k}"] for k in "gbmv"], 1),
        "bn2": np.stack([a[f"L2_gnn_bn2_{k}"] for k in "gbmv"], 1),
        "bih": columns(a["L2_gnn_b_ih"], 3),
        "bhh": columns(a["L2_gnn_b_hh"], 3),
        "bse": bse,
    }
    arrays = {
        "x": a["x"],
        "xT": a["x"].transpose(0, 2, 1),
        "adj": a["adj"],
        "adjT": a["adj"].transpose(0, 2, 1),
        "packed": np.concatenate([parts[name] for name, _ in PARTS], 1),
        "conv2": a["L2_gnn_conv2_w"].transpose(1, 2, 0).reshape(D, TAPS * D),
    }
    arrays = {f"in_{name}": np.ascontiguousarray(v) for name, v in arrays.items()}
    nc = bacc.Bacc("TRN2", target_bir_lowering=False, num_devices=1)
    args = [nc.dram_tensor(name, v.shape, mybir.dt.from_np(v.dtype), kind="ExternalInput").ap() for name, v in arrays.items()]
    args.append(nc.dram_tensor("out", (BATCH, N, D), F32, kind="ExternalOutput").ap())
    gnn_stack_kernel(nc, *args)
    return run_bass_kernel_spmd(nc, [arrays], core_ids=[0]).results[0]["out"]
```

```python
from contextlib import ExitStack

import concourse.bass as bass
from concourse import mybir

F32 = mybir.dt.float32
F32R = mybir.dt.float32r
BF16 = mybir.dt.bfloat16
ALU = mybir.AluOpType
ACT = mybir.ActivationFunctionType
AX_X = mybir.AxisListType.X

P = 128
BATCH = 32
N = 256
D = 128
T = N // P
HEADS = 8
HD = D // HEADS
GH = 4
TAPS = 17
PAD = TAPS // 2
HALF = 64
EPS = 1e-5
MASKED = -1e9

PARTS = [
    ("w0", 3 * D), ("w1", 2 * D), ("w2", 2 * D), ("conv1", D), ("wmsg", D), ("wih", 6 * D), ("whh", 3 * D),
    ("wq", 2 * P), ("wk", 2 * P), ("wv", D), ("wo", D), ("wse", P), ("bt_row", D), ("b2_row", D), ("bmsg_row", D),
    ("we", HEADS), ("ident", P), ("head_rows", GH), ("shift_rows", HEADS), ("eps", 1), ("b1", 2),
    ("bn1", 4), ("bn2", 4), ("bih", 3), ("bhh", 3), ("bse", 1),
]
START, WIDTH, TOTAL = {}, {}, 0
for _name, _width in PARTS:
    START[_name], WIDTH[_name] = TOTAL, _width
    TOTAL += _width


def gnn_stack_kernel(nc, x, xT, adj, adjT, packed, conv2, out):
    ctx = ExitStack()
    with ctx:
        def sb(name, shape, dt=F32):
            return ctx.enter_context(nc.sbuf_tensor(name, shape, dt))

        def sem(name):
            return ctx.enter_context(nc.semaphore(name))

        consts = sb("consts", [P, TOTAL])

        def const(name, lo=0, width=None):
            start = START[name] + lo
            return consts[:, start:start + (WIDTH[name] - lo if width is None else width)]

        conv2_w = sb("conv2_w", [P, TAPS * D])
        conv2_hi = sb("conv2_hi", [P, TAPS * D], F32R)
        conv2_lo = sb("conv2_lo", [P, TAPS * D], F32R)
        ident16 = sb("ident16", [P, P], BF16)
        we_ident = sb("we_ident", [P, HEADS, P], F32R)
        bn_rstd = sb("bn_rstd", [P, 2])
        bn_scale = sb("bn_scale", [P, 2])
        bn_mean = sb("bn_mean", [P, 2])
        bn_bias = sb("bn_bias", [P, 2])
        gate_sum = sb("gate_sum", [P, 2])
        gate_bias = sb("gate_bias", [P, 2])
        one_eps = sb("one_eps", [P, 1])
        minus_half = sb("minus_half", [P, 2])

        x_in = sb("x_in", [P, 2, T, D])
        xT_in = sb("xT_in", [P, 2, N])
        adj_in = sb("adj_in", [P, 2, T, N])
        adjT_in = sb("adjT_in", [P, 2, T, N])
        adjT_att = sb("adjT_att", [P, T * N])
        adj_round = sb("adj_round", [P, 2, T * N], F32R)
        mask = sb("mask", [P, 2, T * N], BF16)
        maskT = sb("maskT", [P, 2, T * N], BF16)

        deg = sb("deg", [P, T])
        deg_eps = sb("deg_eps", [P, T])
        norm = sb("norm", [P, T])
        x_less1 = sb("x_less1", [P, T, D])
        hom_in = sb("hom_in", [P, T, D])
        het = sb("het", [P, T, D])
        gate_pre = sb("gate_pre", [P, T, D])
        gate_tanh = sb("gate_tanh", [P, T, D])
        hom_het = sb("hom_het", [P, T, D])
        gated = sb("gated", [P, T, D])
        mixed = sb("mixed", [P, T, D])
        mixed_exp = sb("mixed_exp", [P, T, D])
        relu_part = sb("relu_part", [P, T, D])
        y = [sb(f"y{k}", [P, T, D]) for k in range(4)]
        stats = [sb(f"stats{k}", [P, T, 6]) for k in range(4)]
        moments = [sb(f"moments{k}", [P, T, 2]) for k in range(4)]
        var_eps = [sb(f"var_eps{k}", [P, T]) for k in range(4)]
        rstd = [sb(f"rstd{k}", [P, T]) for k in range(4)]
        x1 = sb("x1", [P, T, D])
        x1T = sb("x1T", [P, N])
        x1_b2 = sb("x1_b2", [P, T, D])
        hT = sb("hT", [P, N])
        hidT = sb("hidT", [P, 2, N])
        x2 = sb("x2", [P, T, D])
        x2T = sb("x2T", [P, N])
        c1 = sb("c1", [P, N])
        c1_hi = sb("c1_hi", [P, N + 2 * PAD], F32R)
        c1_lo = sb("c1_lo", [P, N + 2 * PAD], F32R)
        dist_l = sb("dist_l", [P, N])
        dist_r = sb("dist_r", [P, N])
        msg_pre = sb("msg_pre", [P, T, D])
        msg = sb("msg", [P, T, D])
        near = sb("near", [P, T * N])
        nearT = sb("nearT", [P, T * N])
        conv_sum = sb("conv_sum", [P, N])
        convT = sb("convT", [P, N])
        nmpT = sb("nmpT", [P, N])
        r_tanh = sb("r_tanh", [P, N])
        z_tanh = sb("z_tanh", [P, N])
        hn_half = sb("hn_half", [P, N])
        r_hn = sb("r_hn", [P, N])
        n_pre = sb("n_pre", [P, N])
        nT = sb("nT", [P, N])
        x_less_n = sb("x_less_n", [P, N])
        z_part = sb("z_part", [P, N])
        n_plus_x = sb("n_plus_x", [P, N])
        y2T = sb("y2T", [P, N])
        x3 = sb("x3", [P, T, D])
        x3T = sb("x3T", [P, N])
        q_hilo = sb("q_hilo", [P, 2, N], F32R)
        q_shift = sb("q_shift", [P, 2, N], F32R)
        k_hi = sb("k_hi", [P, 2, N], F32R)
        k_lo = sb("k_lo", [P, 2, N], F32R)
        kh_head = sb("kh_head", [P, HEADS, N], F32R)
        kl_head = sb("kl_head", [P, HEADS, N], F32R)
        v_one = sb("v_one", [P, T, HEADS, 32])
        maxima = sb("maxima", [P, T, P])
        weights = sb("weights", [P, 3, T * N])
        oT = sb("oT", [P, 2, N])
        inv_sum = sb("inv_sum", [P, T * HEADS])
        o = sb("o", [P, T, D])
        oT_all = sb("oT_all", [P, N])
        result = sb("result", [P, T, D])

        la, lb, lc = (ctx.enter_context(nc.psum_tensor(f"layer_bank{i}", [P, 512], F32)) for i in range(3))
        score = ctx.enter_context(nc.psum_tensor("score_banks", [P, 4, 512], F32))
        att = ctx.enter_context(nc.psum_tensor("att_bank", [P, 512], F32))

        products = """
            const_loaded conv2_loaded setup_dve setup_pool setup_chain pool_chain pool_passed sp_passed dve_passed
            loaded adjT_att stored
            deg deg_eps norm x_less1 proj0 hom_in gate_pre het gate_tanh agg0 hom_het gated mixed mixed_exp relu_part
            x1 x1_pT x1T agg1 hT hid_p hidT out1_p x1_b2
            x2 x2_pT x2T conv1_p c1_hi c1 c1_lo se_p dist_dve dist_act msg_p msg_pre msg dist_p near nearT
            conv2_p conv_sum convT nmp_p nmpT rz_p r_tanh z_tanh gn_p hn_half r_hn n_pre nT x_less_n z_part n_plus_x
            y2T y2_p x3 x3_pT x3T
            q_p q_hi q_lo q_copy k_p k_hi k_lo kh_head kl_head v_p v_one masks s1_p maxima max_pT shift
            s2_p biased weight pv oT o_p inv_sum o o_pT oT_all wo_p result
        """.split()
        ready = {name: sem(f"{name}_ready") for name in products}
        y_ready = [sem(f"y{k}_ready") for k in range(4)]
        stats_ready = [sem(f"stats{k}_ready") for k in range(4)]
        moments_ready = [sem(f"moments{k}_ready") for k in range(4)]
        var_eps_ready = [sem(f"var_eps{k}_ready") for k in range(4)]
        rstd_ready = [sem(f"rstd{k}_ready") for k in range(4)]
        block = ctx.enter_context(nc.Block())

        def wait(eng, semaphore, count):
            if not isinstance(count, int) or count > 0:
                eng.wait_ge(semaphore, count)

        def count(eng, value):
            return value if isinstance(value, int) else eng.snap(value)

        def steps(eng, body):
            body(-1, 1, True, False, False)
            body(0, 0, True, True, False)
            with eng.Fori(0, BATCH // 2 - 1) as i:
                for half in (0, 1):
                    body(i * 2 + (1 + half), 1 - half, True, True, True)
            body(BATCH - 1, 1, False, True, True)
            body(BATCH, 0, False, False, True)

        @block.sync
        def _(sp):
            def load(graph, buf):
                at = bass.ds(graph, 1)
                sp.dma_start(x_in[:, buf], x[at].rearrange("o (t p) d -> p (o t) d", p=P)).then_inc(ready["loaded"], 16)
                sp.dma_start(xT_in[:, buf], xT[at].rearrange("o d n -> d (o n)")).then_inc(ready["loaded"], 16)
                sp.dma_start(adj_in[:, buf], adj[at].rearrange("o (t p) m -> p (o t) m", p=P)).then_inc(ready["loaded"], 16)
                sp.dma_start(adjT_in[:, buf], adjT[at].rearrange("o (t p) n -> p (o t) n", p=P)).then_inc(ready["loaded"], 16)

            def body(s, buf, more, used):
                if more:
                    sp.wait_ge(ready["loaded"], count(sp, (s + 2) * 64))
                    sp.nop().then_inc(ready["sp_passed"], 1)
                    sp.wait_ge(ready["masks"], count(sp, (s + 1) * 3))
                    sp.nop().then_inc(ready["sp_passed"], 1)
                    sp.wait_ge(ready["nearT"], count(sp, s + 1))
                    sp.nop().then_inc(ready["sp_passed"], 1)
                    load(s + 2, buf)
                if used:
                    sp.wait_ge(ready["biased"], count(sp, s * HEADS))
                    sp.nop().then_inc(ready["sp_passed"], 1)
                sp.dma_start(adjT_att[:].rearrange("p (t n) -> p t n", t=T),
                             adjT[bass.ds(s, 1)].rearrange("o (t p) n -> p (o t) n", p=P)).then_inc(ready["adjT_att"], 16)

            sp.nop().then_inc(ready["stored"], 16)
            load(0, 0)
            sp.dma_start(consts[:], packed).then_inc(ready["const_loaded"], 16)
            sp.dma_start(conv2_w[:], conv2).then_inc(ready["conv2_loaded"], 16)
            sp.wait_ge(ready["loaded"], 64)
            load(1, 1)
            body(0, 0, True, False)
            body(1, 1, True, True)
            with sp.Fori(0, BATCH // 2 - 2) as i:
                for half in (0, 1):
                    body(i * 2 + (2 + half), half, True, True)
            body(BATCH - 2, 0, False, True)
            body(BATCH - 1, 1, False, True)
            sp.wait_ge(ready["stored"], 16 * (BATCH + 1))

        @block.gpsimd
        def _(pool):
            links = [0]

            def link(instruction):
                links[0] += 1
                instruction.then_inc(ready["pool_chain"], 1)
                pool.wait_ge(ready["pool_chain"], links[0])

            link(pool.memset(minus_half[:], -0.5))
            pool.wait_ge(ready["const_loaded"], 16)
            for k, bn in enumerate(("bn1", "bn2")):
                link(pool.tensor_scalar(bn_mean[:, k:k + 1], const(bn, 3, 1), EPS, None, ALU.add))
                pool.tensor_tensor(bn_rstd[:, k:k + 1], bn_mean[:, k:k + 1], minus_half[:, 0:1], ALU.pow).then_inc(ready["setup_pool"], 1)

            def layer_norm(k, n, n2):
                pool.wait_ge(moments_ready[k], n2)
                pool.nop().then_inc(ready["pool_passed"], 1)
                pool.tensor_scalar(var_eps[k][:], moments[k][:, :, 1], EPS, None, ALU.add).then_inc(var_eps_ready[k], 1)
                pool.wait_ge(var_eps_ready[k], n)
                pool.tensor_tensor(rstd[k][:], var_eps[k][:], minus_half[:], ALU.pow).then_inc(rstd_ready[k], 1)

            def body(s, buf, front, layers, attention):
                f, n, m = count(pool, s + 2), count(pool, s + 1), count(pool, s)
                f2, n2, m2 = count(pool, s * 2 + 4), count(pool, s * 2 + 2), count(pool, s * 2)
                if layers:
                    pool.wait_ge(ready["x1"], n2)
                    pool.tensor_tensor(x1_b2[:], x1[:], const("b2_row").rearrange("p (o d) -> p o d", o=1).broadcast_to([P, T, D]),
                                       ALU.add).then_inc(ready["x1_b2"], 1)
                if front:
                    pool.wait_ge(ready["deg"], f)
                    pool.nop().then_inc(ready["pool_passed"], 1)
                    pool.tensor_scalar(deg_eps[:], deg[:], 1e-6, None, ALU.add).then_inc(ready["deg_eps"], 1)
                    pool.wait_ge(ready["deg_eps"], f)
                    pool.tensor_tensor(norm[:], deg_eps[:], minus_half[:], ALU.pow).then_inc(ready["norm"], 1)
                if layers:
                    layer_norm(1, n, n2)
                if front:
                    wait(pool, ready["relu_part"], n)
                    pool.nop().then_inc(ready["pool_passed"], 1)
                    pool.tensor_scalar(x_less1[:], x_in[:, 1 - buf], -1.0, None, ALU.add).then_inc(ready["x_less1"], 1)
                if layers:
                    pool.wait_ge(ready["msg_pre"], n)
                    pool.nop().then_inc(ready["pool_passed"], 1)
                    pool.tensor_scalar(msg[:], msg_pre[:], 0.0, None, ALU.max).then_inc(ready["msg"], 1)
                    pool.tensor_scalar(mask[:, buf], adj_in[:, buf].rearrange("p t m -> p (t m)"), 0.0, MASKED,
                                       ALU.is_equal, ALU.mult).then_inc(ready["masks"], 1)
                    pool.tensor_scalar(maskT[:, buf], adjT_in[:, buf].rearrange("p t m -> p (t m)"), 0.0, MASKED,
                                       ALU.is_equal, ALU.mult).then_inc(ready["masks"], 1)
                    pool.tensor_scalar(adj_round[:, buf], adj_in[:, buf].rearrange("p t m -> p (t m)"), 1.0, None,
                                       ALU.mult).then_inc(ready["masks"], 1)
                    pool.wait_ge(ready["nT"], n)
                    pool.tensor_tensor(n_plus_x[:], nT[:], x2T[:], ALU.add).then_inc(ready["n_plus_x"], 1)
                    layer_norm(2, n, n2)
                if attention:
                    layer_norm(3, m, m2)
                if front:
                    layer_norm(0, f, f2)

            steps(pool, body)

        @block.scalar
        def _(act):
            act.wait_ge(ready["setup_dve"], 1)

            def body(s, buf, front, layers, attention):
                f, n, m = count(act, s + 2), count(act, s + 1), count(act, s)

                def high_of_head(h):
                    act.activation(kh_head[:, h], k_hi[:, h // GH].bitcast(F32), ACT.Copy,
                                   scale=const("head_rows", h % GH, 1)).then_inc(ready["kh_head"], 1)

                def exponentials(h):
                    act.wait_ge(ready["biased"], s * HEADS - (HEADS - 1 - h))
                    act.activation(weights[:, h % 3], weights[:, h % 3], ACT.Exp).then_inc(ready["weight"], 1)

                if attention:
                    act.wait_ge(ready["q_p"], m)
                    act.activation(q_hilo[:], score[:, 0].rearrange("p (g n) -> p g n", g=2), ACT.Copy, scale=HD ** -0.5).then_inc(ready["q_hi"], 1)
                    act.wait_ge(ready["k_p"], m)
                    act.activation(k_hi[:], score[:, 1].rearrange("p (g n) -> p g n", g=2), ACT.Copy).then_inc(ready["k_hi"], 1)
                if layers:
                    act.wait_ge(ready["x1_pT"], n)
                    act.activation(x1T[:], la[:, 0:N], ACT.Copy).then_inc(ready["x1T"], 1)
                if attention:
                    act.wait_ge(ready["k_hi"], m)
                    high_of_head(0)
                    high_of_head(1)
                    act.wait_ge(ready["v_p"], m)
                    act.activation(v_one[:, :, :, 0:HD], att[:, 0:N].rearrange("p (t h d) -> p t h d", t=T, h=HEADS), ACT.Copy).then_inc(ready["v_one"], 1)
                if layers:
                    act.wait_ge(ready["hid_p"], n)
                    for k in range(2):
                        act.activation(hidT[:, k], lc[:, k * N:(k + 1) * N], ACT.Relu, bias=const("b1", k, 1)).then_inc(ready["hidT"], 1)
                if attention:
                    for h in range(2, HEADS):
                        high_of_head(h)
                if layers:
                    act.wait_ge(ready["x2_pT"], n)
                    act.activation(x2T[:], la[:, 0:N], ACT.Copy).then_inc(ready["x2T"], 1)
                if attention:
                    act.wait_ge(ready["max_pT"], m)
                    for g in range(2):
                        act.activation(q_shift[HALF:HALF + 32, g], att[HALF:HALF + 32, 0:N], ACT.Copy, scale=-1.0).then_inc(ready["shift"], 1)
                if layers:
                    act.wait_ge(ready["conv1_p"], n)
                    for dst, name in ((c1_hi[:, PAD:PAD + N], "c1_hi"), (c1[:], "c1")):
                        act.activation(dst, lb[:, 0:N], ACT.Relu, bias=bn_bias[:, 0:1], scale=bn_scale[:, 0:1]).then_inc(ready[name], 1)
                    act.wait_ge(ready["se_p"], n)
                    act.activation(dist_r[32:64], lc[32:64, 0:N], ACT.Square, bias=const("bse")[32:64]).then_inc(ready["dist_act"], 1)
                    act.activation(dist_l[64:96], lc[64:96, 0:N], ACT.Square, bias=const("bse")[64:96]).then_inc(ready["dist_act"], 1)
                if attention:
                    exponentials(0)
                    exponentials(1)
                if layers:
                    act.wait_ge(ready["dist_p"], n)
                    act.activation(near[:], lc[:], ACT.Exp, scale=2.0).then_inc(ready["near"], 1)
                if attention:
                    exponentials(2)
                    exponentials(3)
                if layers:
                    act.wait_ge(ready["conv_sum"], n)
                    act.activation(convT[:], conv_sum[:], ACT.Relu, bias=bn_bias[:, 1:2]).then_inc(ready["convT"], 1)
                    act.wait_ge(ready["nmp_p"], n)
                    act.activation(nmpT[:], la[:, 0:N], ACT.Copy).then_inc(ready["nmpT"], 1)
                if attention:
                    exponentials(4)
                    exponentials(5)
                if layers:
                    act.wait_ge(ready["rz_p"], n)
                    act.activation(r_tanh[:], lc[:, 0:N], ACT.Tanh, bias=gate_bias[:, 0:1], scale=0.5).then_inc(ready["r_tanh"], 1)
                    act.activation(z_tanh[:], lc[:, N:2 * N], ACT.Tanh, bias=gate_bias[:, 1:2], scale=0.5).then_inc(ready["z_tanh"], 1)
                if attention:
                    exponentials(6)
                if layers:
                    act.wait_ge(ready["n_pre"], n)
                    act.activation(nT[:], n_pre[:], ACT.Tanh, bias=const("bih", 2, 1)).then_inc(ready["nT"], 1)
                if attention:
                    exponentials(7)
                if front:
                    act.wait_ge(ready["proj0"], f)
                    act.wait_ge(ready["norm"], f)
                    for t in range(T):
                        act.activation(hom_in[:, t], score[:, 2 + t, 0:D], ACT.Copy, scale=norm[:, t:t + 1]).then_inc(ready["hom_in"], 1)
                if attention:
                    act.wait_ge(ready["pv"], s * HEADS)
                    act.activation(oT[:], att[:].rearrange("p (g n) -> p g n", g=2), ACT.Copy).then_inc(ready["oT"], 1)
                if front:
                    act.wait_ge(ready["gate_pre"], f)
                    act.activation(gate_tanh[:], gate_pre[:], ACT.Tanh, scale=0.5).then_inc(ready["gate_tanh"], 1)
                if attention:
                    act.wait_ge(ready["o_pT"], m)
                    act.activation(oT_all[:], score[:, 1, 0:N], ACT.Copy).then_inc(ready["oT_all"], 1)
                if front:
                    act.wait_ge(ready["mixed"], f)
                    act.activation(mixed_exp[:], mixed[:], ACT.Exp).then_inc(ready["mixed_exp"], 1)
                if layers:
                    act.wait_ge(ready["x3_pT"], n)
                    act.activation(x3T[:], lc[:, 0:N], ACT.Copy).then_inc(ready["x3T"], 1)
                if attention:
                    act.wait_ge(ready["result"], s * 2)
                    act.dma_start(out[bass.ds(s - 1, 1)].rearrange("o (t p) d -> p (o t) d", p=P), result[:]).then_inc(ready["stored"], 16)

            steps(act, body)

        @block.vector
        def _(dve):
            links = [0]

            def link(instruction):
                links[0] += 1
                instruction.then_inc(ready["setup_chain"], 1)
                dve.wait_ge(ready["setup_chain"], links[0])

            link(dve.memset(c1_hi[:].bitcast(F32), 0.0))
            link(dve.memset(c1_lo[:].bitcast(F32), 0.0))
            link(dve.memset(maxima[:], 0.0))
            link(dve.memset(q_shift[:].bitcast(F32), 0.0))
            link(dve.memset(kl_head[:].bitcast(F32), 0.0))
            link(dve.memset(v_one[:], 0.0))
            link(dve.memset(v_one[:, :, :, HD:HD + 1], 1.0))
            link(dve.memset(dist_l[32:64], -0.5))
            link(dve.memset(dist_r[64:96], -0.5))
            dve.wait_ge(ready["const_loaded"], 16)
            link(dve.tensor_copy(ident16[:], const("ident")))
            for h in range(HEADS):
                link(dve.tensor_scalar(we_ident[:, h], const("ident"), const("we", h, 1), None, ALU.mult))
                link(dve.tensor_scalar(kl_head[HALF:P, h], kl_head[HALF:P, h].bitcast(F32), const("shift_rows", h, 1)[HALF:P], None, ALU.add))
            dve.wait_ge(ready["setup_pool"], 2)
            for k, bn in enumerate(("bn1", "bn2")):
                link(dve.tensor_tensor(bn_scale[:, k:k + 1], bn_rstd[:, k:k + 1], const(bn, 0, 1), ALU.mult))
                link(dve.tensor_tensor(bn_mean[:, k:k + 1], const(bn, 2, 1), bn_scale[:, k:k + 1], ALU.mult))
                link(dve.tensor_tensor(bn_bias[:, k:k + 1], const(bn, 1, 1), bn_mean[:, k:k + 1], ALU.subtract))
            link(dve.tensor_tensor(gate_sum[:], const("bih", 0, 2), const("bhh", 0, 2), ALU.add))
            link(dve.tensor_scalar(gate_bias[:], gate_sum[:], 0.5, None, ALU.mult))
            link(dve.tensor_scalar(one_eps[:], const("eps"), 1.0, None, ALU.add))
            dve.wait_ge(ready["conv2_loaded"], 16)
            link(dve.tensor_copy(conv2_hi[:], conv2_w[:]))
            link(dve.tensor_tensor(conv2_lo[:], conv2_w[:], conv2_hi[:].bitcast(F32), ALU.subtract))
            dve.nop().then_inc(y_ready[3], 1)
            dve.nop().then_inc(ready["setup_dve"], 1)

            def moments_of(k, n2, src):
                for t in range(T):
                    dve.bn_stats(stats[k][:, t], src(t)).then_inc(stats_ready[k], 1)
                dve.wait_ge(stats_ready[k], n2)
                dve.nop().then_inc(ready["dve_passed"], 1)
                for t in range(T):
                    dve.bn_aggr(moments[k][:, t], stats[k][:, t]).then_inc(moments_ready[k], 1)

            def normalise(k, n, n2, dst, src, name):
                dve.wait_ge(moments_ready[k], n2)
                dve.wait_ge(rstd_ready[k], n)
                for t in range(T):
                    dve.tensor_scalar(dst[:, t], src(t), moments[k][:, t, 0:1], rstd[k][:, t:t + 1],
                                      ALU.subtract, ALU.mult).then_inc(ready[name], 1)

            def body(s, buf, front, layers, attention):
                f, n, m = count(dve, s + 2), count(dve, s + 1), count(dve, s)
                f2, n2, m2 = count(dve, s * 2 + 4), count(dve, s * 2 + 2), count(dve, s * 2)
                heads = [s * HEADS - (HEADS - 1 - h) for h in range(HEADS)]

                def maximum(pair):
                    dve.wait_ge(ready["s1_p"], s * 4 - (3 - pair))
                    banks = score[:, 2 * (pair % 2):2 * (pair % 2) + 2].rearrange("p h (t j) -> p h t j", t=T)
                    dst = maxima[:, :, HALF + 2 * pair:HALF + 2 * pair + 2].rearrange("p t h -> p h t")
                    dve.tensor_reduce(dst, banks, AX_X, ALU.max).then_inc(ready["maxima"], 1)

                def low_of_head(h):
                    dve.tensor_scalar(kl_head[0:HALF, h], k_lo[0:HALF, h // GH].bitcast(F32),
                                      const("head_rows", h % GH, 1)[0:HALF], None, ALU.mult).then_inc(ready["kl_head"], 1)

                def bias(h):
                    dve.wait_ge(ready["s2_p"], heads[h])
                    if h >= 3:
                        dve.wait_ge(ready["pv"], heads[h - 3])
                    dve.scalar_tensor_tensor(out=weights[:, h % 3], in0=adjT_att[:], scalar=const("we", h, 1), in1=score[:, h % 4],
                                             op0=ALU.mult, op1=ALU.add).then_inc(ready["biased"], 1)

                if attention:
                    dve.wait_ge(ready["q_hi"], m)
                    dve.scalar_tensor_tensor(out=q_hilo[HALF:P], in0=score[HALF:P, 0].rearrange("p (g n) -> p g n", g=2), scalar=HD ** -0.5,
                                             in1=q_hilo[HALF:P].bitcast(F32), op0=ALU.mult, op1=ALU.subtract).then_inc(ready["q_lo"], 1)
                    dve.tensor_copy(q_shift[0:HALF], q_hilo[0:HALF].bitcast(F32)).then_inc(ready["q_copy"], 1)
                    dve.wait_ge(ready["k_hi"], m)
                    dve.tensor_tensor(k_lo[0:HALF], score[0:HALF, 1].rearrange("p (g n) -> p g n", g=2), k_hi[0:HALF].bitcast(F32),
                                      ALU.subtract).then_inc(ready["k_lo"], 1)
                if front:
                    dve.wait_ge(ready["loaded"], s * 64 + 128)
                    dve.tensor_reduce(deg[:], adj_in[:, 1 - buf], AX_X, ALU.add).then_inc(ready["deg"], 1)
                if layers:
                    dve.wait_ge(ready["agg1"], n)
                    dve.wait_ge(ready["x1T"], n)
                    dve.scalar_tensor_tensor(out=hT[:], in0=x1T[:], scalar=one_eps[:], in1=lb[:, 0:N], op0=ALU.mult,
                                             op1=ALU.add).then_inc(ready["hT"], 1)
                if attention:
                    maximum(0)
                if layers:
                    dve.wait_ge(ready["out1_p"], n)
                    dve.wait_ge(ready["x1_b2"], n)
                    dve.tensor_tensor(y[1][:], lb[:, 0:N].rearrange("p (t d) -> p t d", t=T), x1_b2[:], ALU.add).then_inc(y_ready[1], 1)
                    dve.wait_ge(y_ready[1], n)
                    moments_of(1, n2, lambda t: y[1][:, t])
                if attention:
                    maximum(1)
                if layers:
                    normalise(1, n, n2, x2, lambda t: y[1][:, t], "x2")
                if attention:
                    maximum(2)
                    dve.wait_ge(ready["k_lo"], m)
                    for h in range(0, 4):
                        low_of_head(h)
                    maximum(3)
                    for h in range(4, HEADS):
                        low_of_head(h)
                if layers:
                    dve.wait_ge(ready["se_p"], n)
                    for dst in (dist_l, dist_r):
                        dve.tensor_scalar(dst[0:32], lc[0:32, 0:N], const("bse")[0:32], None, ALU.add).then_inc(ready["dist_dve"], 1)
                    dve.wait_ge(ready["msg_p"], n)
                    dve.tensor_tensor(msg_pre[:], la[:, 0:N].rearrange("p (t d) -> p t d", t=T),
                                      const("bmsg_row").rearrange("p (o d) -> p o d", o=1).broadcast_to([P, T, D]), ALU.add
                                      ).then_inc(ready["msg_pre"], 1)
                    dve.wait_ge(ready["c1"], n)
                    dve.wait_ge(ready["c1_hi"], n)
                    dve.tensor_tensor(c1_lo[:, PAD:PAD + N], c1[:], c1_hi[:, PAD:PAD + N].bitcast(F32), ALU.subtract).then_inc(ready["c1_lo"], 1)
                if attention:
                    dve.wait_ge(ready["adjT_att"], s * 16)
                    bias(0)
                    bias(1)
                if layers:
                    dve.wait_ge(ready["near"], n)
                    dve.tensor_tensor(nearT[:], near[:], adjT_in[:, buf].rearrange("p t n -> p (t n)"), ALU.mult).then_inc(ready["nearT"], 1)
                if attention:
                    bias(2)
                    bias(3)
                if layers:
                    dve.wait_ge(ready["conv2_p"], n)
                    dve.scalar_tensor_tensor(out=conv_sum[:], in0=lb[:, 0:N], scalar=bn_scale[:, 1:2], in1=x2T[:], op0=ALU.mult,
                                             op1=ALU.add).then_inc(ready["conv_sum"], 1)
                if attention:
                    bias(4)
                    bias(5)
                if layers:
                    dve.wait_ge(ready["gn_p"], n)
                    dve.tensor_scalar(hn_half[:], lb[:, N:2 * N], const("bhh", 2, 1), 0.5, ALU.add, ALU.mult).then_inc(ready["hn_half"], 1)
                    dve.wait_ge(ready["hn_half"], n)
                    dve.wait_ge(ready["r_tanh"], n)
                    dve.scalar_tensor_tensor(out=r_hn[:], in0=r_tanh[:], scalar=1.0, in1=hn_half[:], op0=ALU.add,
                                             op1=ALU.mult).then_inc(ready["r_hn"], 1)
                    dve.wait_ge(ready["r_hn"], n)
                    dve.tensor_tensor(n_pre[:], lb[:, 0:N], r_hn[:], ALU.add).then_inc(ready["n_pre"], 1)
                if attention:
                    bias(6)
                    bias(7)
                if layers:
                    dve.wait_ge(ready["nT"], n)
                    dve.tensor_tensor(x_less_n[:], x2T[:], nT[:], ALU.subtract).then_inc(ready["x_less_n"], 1)
                    dve.wait_ge(ready["x_less_n"], n)
                    dve.wait_ge(ready["z_tanh"], n)
                    dve.scalar_tensor_tensor(out=z_part[:], in0=z_tanh[:], scalar=1.0, in1=x_less_n[:], op0=ALU.add,
                                             op1=ALU.mult).then_inc(ready["z_part"], 1)
                    dve.wait_ge(ready["z_part"], n)
                    dve.wait_ge(ready["n_plus_x"], n)
                    dve.scalar_tensor_tensor(out=y2T[:], in0=z_part[:], scalar=0.5, in1=n_plus_x[:], op0=ALU.mult,
                                             op1=ALU.add).then_inc(ready["y2T"], 1)
                if front:
                    dve.wait_ge(ready["hom_in"], f2)
                    dve.tensor_tensor(gate_pre[:], score[:, 2:4, 2 * D:3 * D],
                                      const("bt_row").rearrange("p (o d) -> p o d", o=1).broadcast_to([P, T, D]), ALU.add
                                      ).then_inc(ready["gate_pre"], 1)
                    dve.tensor_copy(het[:], score[:, 2:4, D:2 * D]).then_inc(ready["het"], 1)
                if layers:
                    dve.wait_ge(ready["y2_p"], n)
                    moments_of(2, n2, lambda t: la[:, t * D:(t + 1) * D])
                if attention:
                    dve.wait_ge(ready["o_p"], m)
                    by_head = score[:, 0].rearrange("p (a c) -> p a c", c=32)
                    dve.reciprocal(inv_sum[:].rearrange("p (a o) -> p a o", o=1), by_head[:, :, HD:HD + 1]).then_inc(ready["inv_sum"], 1)
                    dve.wait_ge(ready["inv_sum"], m)
                    dve.tensor_tensor(o[:].rearrange("p t (h d) -> p (t h) d", d=HD), by_head[:, :, 0:HD],
                                      inv_sum[:].rearrange("p (a o) -> p a o", o=1).broadcast_to([P, T * HEADS, HD]), ALU.mult
                                      ).then_inc(ready["o"], 1)
                if layers and not attention:
                    normalise(2, n, n2, x3, lambda t: la[:, t * D:(t + 1) * D], "x3")
                if front:
                    dve.wait_ge(ready["agg0"], f)
                    dve.wait_ge(ready["het"], f)
                    for t in range(T):
                        dve.scalar_tensor_tensor(out=hom_het[:, t], in0=att[:, t * D:(t + 1) * D], scalar=norm[:, t:t + 1], in1=het[:, t],
                                                 op0=ALU.mult, op1=ALU.subtract).then_inc(ready["hom_het"], 1)
                    dve.wait_ge(ready["hom_het"], f2)
                    dve.wait_ge(ready["gate_tanh"], f)
                    dve.scalar_tensor_tensor(out=gated[:], in0=gate_tanh[:], scalar=1.0, in1=hom_het[:], op0=ALU.add,
                                             op1=ALU.mult).then_inc(ready["gated"], 1)
                    dve.wait_ge(ready["gated"], f)
                    dve.scalar_tensor_tensor(out=mixed[:], in0=gated[:], scalar=0.5, in1=het[:], op0=ALU.mult,
                                             op1=ALU.add).then_inc(ready["mixed"], 1)
                if attention:
                    dve.wait_ge(ready["wo_p"], m)
                    dve.tensor_tensor(y[3][:], score[:, 1, N:2 * N].rearrange("p (t d) -> p t d", t=T), x3[:], ALU.add).then_inc(y_ready[3], 1)
                    dve.wait_ge(y_ready[3], n)
                if layers and attention:
                    normalise(2, n, n2, x3, lambda t: la[:, t * D:(t + 1) * D], "x3")
                if attention:
                    moments_of(3, m2, lambda t: y[3][:, t])
                if front:
                    dve.wait_ge(ready["mixed"], f)
                    dve.wait_ge(ready["x_less1"], f)
                    dve.scalar_tensor_tensor(out=relu_part[:], in0=mixed[:], scalar=0.0, in1=x_less1[:], op0=ALU.max,
                                             op1=ALU.add).then_inc(ready["relu_part"], 1)
                    dve.wait_ge(ready["relu_part"], f)
                    dve.wait_ge(ready["mixed_exp"], f)
                    dve.scalar_tensor_tensor(out=y[0][:], in0=mixed_exp[:], scalar=1.0, in1=relu_part[:], op0=ALU.min,
                                             op1=ALU.add).then_inc(y_ready[0], 1)
                    dve.wait_ge(y_ready[0], f)
                    moments_of(0, f2, lambda t: y[0][:, t])
                if attention:
                    dve.wait_ge(ready["stored"], s * 16)
                    normalise(3, m, m2, result, lambda t: y[3][:, t], "result")
                if front:
                    normalise(0, f, f2, x1, lambda t: y[0][:, t], "x1")

            steps(dve, body)

        @block.tensor
        def _(pe):
            pe.wait_ge(ready["setup_dve"], 1)

            def turn(dst, src, name):
                for t in range(T):
                    last = pe.transpose(dst[:, t * P:(t + 1) * P], src(t), const("ident"))
                last.then_inc(ready[name], 1)

            def body(s, buf, front, layers, attention):
                f, n, m = count(pe, s + 2), count(pe, s + 1), count(pe, s)
                n2 = count(pe, s * 2 + 2)
                heads = [s * HEADS - (HEADS - 1 - h) for h in range(HEADS)]

                def scores_for_maxima(pair):
                    for h in (2 * pair, 2 * pair + 1):
                        bank = score[:, h % 4]
                        pe.matmul(bank, ident16[:], mask[:, 1 - buf], start=True, stop=False)
                        pe.matmul(bank, we_ident[:, h], adj_round[:, 1 - buf], start=False, stop=False)
                        pe.wait_ge(ready["kh_head"], heads[h])
                        for t in range(T):
                            last = pe.matmul(bank[:, t * N:(t + 1) * N], q_hilo[:, h // GH, t * P:(t + 1) * P], kh_head[:, h],
                                             start=False, stop=t == T - 1)
                    last.then_inc(ready["s1_p"], 1)

                def scores(h):
                    if h >= 4:
                        pe.wait_ge(ready["biased"], heads[h - 4])
                    bank = score[:, h % 4]
                    pe.matmul(bank, ident16[:], maskT[:, 1 - buf], start=True, stop=False)
                    pe.wait_ge(ready["kl_head"], heads[h])
                    for t in range(T):
                        cols = bank[:, t * N:(t + 1) * N]
                        pe.matmul(cols, kh_head[:, h, t * P:(t + 1) * P], q_hilo[:, h // GH], start=False, stop=False)
                        last = pe.matmul(cols, kl_head[:, h, t * P:(t + 1) * P], q_shift[:, h // GH], start=False, stop=t == T - 1)
                    last.then_inc(ready["s2_p"], 1)

                def weigh(h):
                    pe.wait_ge(ready["weight"], heads[h])
                    rows = 32 * (h % GH)
                    for t in range(T):
                        last = pe.matmul(att[rows:rows + 32, (h // GH) * N:(h // GH + 1) * N], v_one[:, t, h],
                                         weights[:, h % 3, t * N:(t + 1) * N], start=t == 0, stop=t == T - 1)
                    last.then_inc(ready["pv"], 1)

                if attention:
                    pe.wait_ge(ready["x3T"], m)
                    pe.wait_ge(y_ready[3], s)
                    for dst, w, name in ((score[:, 0], "wq", "q_p"), (score[:, 1], "wk", "k_p")):
                        for g in range(2):
                            last = pe.matmul(dst[:, g * N:(g + 1) * N], const(w, g * P, P), x3T[:], start=True, stop=True)
                        last.then_inc(ready[name], 1)
                if layers:
                    pe.wait_ge(ready["x1"], n2)
                    turn(la, lambda t: x1[:, t], "x1_pT")
                    for k in range(T):
                        last = pe.matmul(lb[:, 0:N], x1[:, k], adjT_in[:, buf, k], start=k == 0, stop=k == T - 1)
                    last.then_inc(ready["agg1"], 1)
                if attention:
                    if layers:
                        pe.wait_ge(ready["hom_het"], n2)
                    for t in range(T):
                        last = pe.matmul(att[:, t * D:(t + 1) * D], x3T[:, t * P:(t + 1) * P], const("wv"), start=True, stop=True)
                    last.then_inc(ready["v_p"], 1)
                if layers:
                    pe.wait_ge(ready["hT"], n)
                    for k in range(2):
                        last = pe.matmul(lc[:, k * N:(k + 1) * N], const("w1", k * P, P), hT[:], start=True, stop=True)
                    last.then_inc(ready["hid_p"], 1)
                if attention:
                    pe.wait_ge(ready["masks"], s * 3)
                    pe.wait_ge(ready["q_lo"], m)
                    pe.wait_ge(ready["k_lo"], m)
                    scores_for_maxima(0)
                if layers:
                    pe.wait_ge(ready["hidT"], n2)
                    for t in range(T):
                        for k in range(2):
                            last = pe.matmul(lb[:, t * D:(t + 1) * D], hidT[:, k, t * P:(t + 1) * P], const("w2", k * D, D),
                                             start=k == 0, stop=k == 1)
                    last.then_inc(ready["out1_p"], 1)
                if attention:
                    scores_for_maxima(1)
                    pe.wait_ge(ready["maxima"], s * 4 - 3)
                    scores_for_maxima(2)
                if layers:
                    pe.wait_ge(ready["x2"], n2)
                    turn(la, lambda t: x2[:, t], "x2_pT")
                if attention:
                    pe.wait_ge(ready["maxima"], s * 4 - 2)
                    scores_for_maxima(3)
                if layers:
                    pe.wait_ge(ready["x2T"], n)
                    pe.matmul(lb[:, 0:N], const("conv1"), x2T[:], start=True, stop=True).then_inc(ready["conv1_p"], 1)
                    pe.matmul(lc[:, 0:N], const("wse"), x2T[:], start=True, stop=True).then_inc(ready["se_p"], 1)
                    for t in range(T):
                        last = pe.matmul(la[:, t * D:(t + 1) * D], x2T[:, t * P:(t + 1) * P], const("wmsg"), start=True, stop=True)
                    last.then_inc(ready["msg_p"], 1)
                if attention:
                    pe.wait_ge(ready["maxima"], s * 4)
                    pe.wait_ge(ready["v_one"], m)
                    turn(att, lambda t: maxima[:, t], "max_pT")
                    pe.wait_ge(ready["shift"], s * 2)
                    pe.wait_ge(ready["q_copy"], m)
                    scores(0)
                if layers:
                    pe.wait_ge(ready["dist_dve"], n2)
                    pe.wait_ge(ready["dist_act"], n2)
                    for t in range(T):
                        last = pe.matmul(lc[:, t * N:(t + 1) * N], dist_l[0:96, t * P:(t + 1) * P], dist_r[0:96], start=True, stop=True)
                    last.then_inc(ready["dist_p"], 1)
                if attention:
                    scores(1)
                    scores(2)
                    weigh(0)
                    scores(3)
                    weigh(1)
                if layers:
                    pe.wait_ge(ready["c1_lo"], n)
                    for k in range(TAPS):
                        for j, (w, c) in enumerate(((conv2_hi, c1_hi), (conv2_hi, c1_lo), (conv2_lo, c1_hi))):
                            last = pe.matmul(lb[:, 0:N], w[:, k * D:(k + 1) * D], c[:, k:k + N],
                                             start=k == 0 and j == 0, stop=k == TAPS - 1 and j == 2)
                    last.then_inc(ready["conv2_p"], 1)
                    pe.wait_ge(ready["msg"], n)
                    pe.wait_ge(ready["nearT"], n)
                    for k in range(T):
                        last = pe.matmul(la[:, 0:N], msg[:, k], nearT[:, k * N:(k + 1) * N], start=k == 0, stop=k == T - 1)
                    last.then_inc(ready["nmp_p"], 1)
                if attention:
                    scores(4)
                    weigh(2)
                    scores(5)
                    weigh(3)
                if layers:
                    pe.wait_ge(ready["nmpT"], n)
                    pe.wait_ge(ready["convT"], n)
                    for g in range(2):
                        dst = lc[:, g * N:(g + 1) * N]
                        pe.matmul(dst, const("whh", g * D, D), x2T[:], start=True, stop=False)
                        pe.matmul(dst, const("wih", 3 * D + g * D, D), nmpT[:], start=False, stop=False)
                        last = pe.matmul(dst, const("wih", g * D, D), convT[:], start=False, stop=True)
                    last.then_inc(ready["rz_p"], 1)
                    pe.matmul(lb[:, N:2 * N], const("whh", 2 * D, D), x2T[:], start=True, stop=True)
                    pe.matmul(lb[:, 0:N], const("wih", 5 * D, D), nmpT[:], start=True, stop=False)
                    pe.matmul(lb[:, 0:N], const("wih", 2 * D, D), convT[:], start=False, stop=True).then_inc(ready["gn_p"], 1)
                if attention:
                    scores(6)
                    weigh(4)
                    scores(7)
                    weigh(5)
                    weigh(6)
                if front:
                    pe.wait_ge(ready["loaded"], s * 64 + 128)
                    wait(pe, ready["biased"], s * HEADS)
                    for t in range(T):
                        last = pe.matmul(score[:, 2 + t, 0:3 * D], xT_in[:, 1 - buf, t * P:(t + 1) * P], const("w0"), start=True, stop=True)
                    last.then_inc(ready["proj0"], 1)
                if attention:
                    weigh(7)
                    pe.wait_ge(ready["oT"], m)
                    for t in range(T):
                        for g in range(2):
                            last = pe.transpose(score[:, 0, (2 * t + g) * P:(2 * t + g + 1) * P], oT[:, g, t * P:(t + 1) * P], const("ident"))
                    last.then_inc(ready["o_p"], 1)
                if front:
                    pe.wait_ge(ready["hom_in"], s * 2 + 4)
                    for t in range(T):
                        for k in range(T):
                            last = pe.matmul(att[:, t * D:(t + 1) * D], adjT_in[:, 1 - buf, k, t * P:(t + 1) * P], hom_in[:, k],
                                             start=k == 0, stop=k == T - 1)
                    last.then_inc(ready["agg0"], 1)
                if layers:
                    pe.wait_ge(ready["y2T"], n)
                    turn(la, lambda t: y2T[:, t * P:(t + 1) * P], "y2_p")
                if attention:
                    pe.wait_ge(ready["o"], m)
                    turn(score[:, 1], lambda t: o[:, t], "o_pT")
                    pe.wait_ge(ready["oT_all"], m)
                    for t in range(T):
                        last = pe.matmul(score[:, 1, N + t * D:N + (t + 1) * D], oT_all[:, t * P:(t + 1) * P], const("wo"), start=True, stop=True)
                    last.then_inc(ready["wo_p"], 1)
                if layers:
                    pe.wait_ge(ready["x3"], n2)
                    turn(lc, lambda t: x3[:, t], "x3_pT")

            steps(pe, body)


def kernel(**inputs):
    import numpy as np
    import concourse.bacc as bacc
    from concourse.bass_utils import run_bass_kernel_spmd

    a = {name: np.asarray(v) for name, v in inputs.items()}

    def column(v, rows=P):
        return np.broadcast_to(v.reshape(1, -1), (rows, v.size))

    def columns(v, k):
        return v.reshape(k, P).T

    w_se, b_se = a["L2_gnn_w_se"], a["L2_gnn_b_se"]
    wse = np.zeros((D, P), w_se.dtype)
    bse = np.zeros((P, 1), b_se.dtype)
    for start in (0, 32, 64):
        wse[:, start:start + 3] = w_se.T
        bse[start:start + 3, 0] = b_se
    head_rows = np.zeros((P, GH), np.float32)
    shift_rows = np.zeros((P, HEADS), np.float32)
    for h in range(GH):
        for start in (0, HALF):
            head_rows[start + h * HD:start + (h + 1) * HD, h] = 1.0
    for h in range(HEADS):
        shift_rows[HALF + h, h] = 1.0
    twice = lambda w: np.concatenate([w[:, :HALF], w[:, :HALF], w[:, HALF:], w[:, HALF:]], 1)
    tiles = lambda w: np.concatenate(np.split(w, w.shape[0] // P, 0), 1)
    parts = {
        "w0": np.concatenate([a["L0_gnn_theta"], a["L0_gnn_W_h"], a["L0_gnn_W_t"]], 1),
        "w1": a["L1_gnn_W1"],
        "w2": tiles(a["L1_gnn_W2"]),
        "conv1": a["L2_gnn_conv1_w"][:, :, 0].T,
        "wmsg": a["L2_gnn_w_msg"].T,
        "wih": tiles(a["L2_gnn_w_ih"].T),
        "whh": a["L2_gnn_w_hh"].T,
        "wq": twice(a["L3_gnn_W_q"].T),
        "wk": twice(a["L3_gnn_W_k"].T),
        "wv": a["L3_gnn_W_v"].T,
        "wo": a["L3_gnn_W_o"].T,
        "wse": wse,
        "bt_row": column(a["L0_gnn_b_t"]),
        "b2_row": column(a["L1_gnn_b2"]),
        "bmsg_row": column(a["L2_gnn_b_msg"]),
        "we": column(a["L3_gnn_W_e"]),
        "ident": np.eye(P, dtype=np.float32),
        "head_rows": head_rows,
        "shift_rows": shift_rows,
        "eps": column(a["L1_gnn_eps"]),
        "b1": columns(a["L1_gnn_b1"], 2),
        "bn1": np.stack([a[f"L2_gnn_bn1_{k}"] for k in "gbmv"], 1),
        "bn2": np.stack([a[f"L2_gnn_bn2_{k}"] for k in "gbmv"], 1),
        "bih": columns(a["L2_gnn_b_ih"], 3),
        "bhh": columns(a["L2_gnn_b_hh"], 3),
        "bse": bse,
    }
    arrays = {
        "x": a["x"],
        "xT": a["x"].transpose(0, 2, 1),
        "adj": a["adj"],
        "adjT": a["adj"].transpose(0, 2, 1),
        "packed": np.concatenate([parts[name] for name, _ in PARTS], 1),
        "conv2": a["L2_gnn_conv2_w"].transpose(1, 2, 0).reshape(D, TAPS * D),
    }
    arrays = {f"in_{name}": np.ascontiguousarray(v) for name, v in arrays.items()}
    nc = bacc.Bacc("TRN2", target_bir_lowering=False, num_devices=1)
    args = [nc.dram_tensor(name, v.shape, mybir.dt.from_np(v.dtype), kind="ExternalInput").ap() for name, v in arrays.items()]
    args.append(nc.dram_tensor("out", (BATCH, N, D), F32, kind="ExternalOutput").ap())
    gnn_stack_kernel(nc, *args)
    return run_bass_kernel_spmd(nc, [arrays], core_ids=[0]).results[0]["out"]
```

```python
from contextlib import ExitStack

import concourse.bass as bass
from concourse import mybir

F32 = mybir.dt.float32
F32R = mybir.dt.float32r
BF16 = mybir.dt.bfloat16
ALU = mybir.AluOpType
ACT = mybir.ActivationFunctionType
AX_X = mybir.AxisListType.X

P = 128
BATCH = 32
N = 256
D = 128
T = N // P
HEADS = 8
HD = D // HEADS
GH = 4
TAPS = 17
PAD = TAPS // 2
HALF = 64
EPS = 1e-5
MASKED = -1e9

PARTS = [
    ("conv1", D), ("wih", 6 * D), ("whh", 3 * D), ("wse", P), ("wq", 2 * P), ("wk", 2 * P),
    ("w0", 3 * D), ("w1", 2 * D), ("w2", 2 * D), ("wmsg", D),
    ("wv", D), ("wo", D), ("het_bt_row", 2 * D), ("b2_row", D), ("bmsg_row", D),
    ("we", HEADS), ("ident", P), ("head_rows", GH), ("shift_rows", HEADS), ("eps", 1), ("b1", 2),
    ("bn1", 4), ("bn2", 4), ("bih", 3), ("bhh", 3), ("bse", 1),
]
START, WIDTH, TOTAL = {}, {}, 0
for _name, _width in PARTS:
    START[_name], WIDTH[_name] = TOTAL, _width
    TOTAL += _width
SPLIT = START["w0"]


def gnn_stack_kernel(nc, x, xT, adj, adjT, packed, conv2, out):
    ctx = ExitStack()
    with ctx:
        def sb(name, shape, dt=F32):
            return ctx.enter_context(nc.sbuf_tensor(name, shape, dt))

        def sem(name):
            return ctx.enter_context(nc.semaphore(name))

        consts = sb("consts", [P, TOTAL])

        def const(name, lo=0, width=None):
            start = START[name] + lo
            return consts[:, start:start + (WIDTH[name] - lo if width is None else width)]

        w_hi = sb("w_hi", [P, SPLIT], F32R)
        w_lo = sb("w_lo", [P, SPLIT], F32R)

        def product(pe, dst, name, lo, parts, start=True, stop=True):
            hi, low = parts
            cols = slice(START[name] + lo, START[name] + lo + P)
            pe.matmul(dst, w_hi[:, cols], hi[:], start=start, stop=False)
            pe.matmul(dst, w_lo[:, cols], hi[:], start=False, stop=False)
            return pe.matmul(dst, w_hi[:, cols], low[:], start=False, stop=stop)

        conv2_w = sb("conv2_w", [P, TAPS * D])
        conv2_hi = sb("conv2_hi", [P, TAPS * D], F32R)
        conv2_lo = sb("conv2_lo", [P, TAPS * D], F32R)
        ident16 = sb("ident16", [P, P], BF16)
        we_ident = sb("we_ident", [P, HEADS, P], F32R)
        bn_rstd = sb("bn_rstd", [P, 2])
        bn_scale = sb("bn_scale", [P, 2])
        bn_mean = sb("bn_mean", [P, 2])
        bn_bias = sb("bn_bias", [P, 2])
        gate_sum = sb("gate_sum", [P, 2])
        gate_bias = sb("gate_bias", [P, 2])
        one_eps = sb("one_eps", [P, 1])
        minus_half = sb("minus_half", [P, 2])

        x_in = sb("x_in", [P, 2, T, D])
        xT_in = sb("xT_in", [P, 2, N])
        adj_in = sb("adj_in", [P, 2, T, N])
        adjT_in = sb("adjT_in", [P, 2, T, N])
        adjT_att = sb("adjT_att", [P, T * N])
        adj_round = sb("adj_round", [P, 2, T * N], F32R)
        mask = sb("mask", [P, 2, T * N], BF16)
        maskT = sb("maskT", [P, 2, T * N], BF16)

        deg = sb("deg", [P, T])
        deg_eps = sb("deg_eps", [P, T])
        norm = sb("norm", [P, T])
        x_less1 = sb("x_less1", [P, T, D])
        hom_in = sb("hom_in", [P, T, D])
        gate_het = sb("gate_het", [P, T, 2 * D])
        gate_tanh = sb("gate_tanh", [P, T, D])
        hom_het = sb("hom_het", [P, T, D])
        gated = sb("gated", [P, T, D])
        mixed = sb("mixed", [P, T, D])
        mixed_exp = sb("mixed_exp", [P, T, D])
        relu_part = sb("relu_part", [P, T, D])
        y = [sb(f"y{k}", [P, T, D]) for k in range(4)]
        stats = [sb(f"stats{k}", [P, T, 6]) for k in range(4)]
        moments = [sb(f"moments{k}", [P, T, 2]) for k in range(4)]
        var_eps = [sb(f"var_eps{k}", [P, T]) for k in range(4)]
        rstd = [sb(f"rstd{k}", [P, T]) for k in range(4)]
        x1 = sb("x1", [P, T, D])
        x1T = sb("x1T", [P, N])
        x1_b2 = sb("x1_b2", [P, T, D])
        hT = sb("hT", [P, N])
        hidT = sb("hidT", [P, 2, N])
        x2 = sb("x2", [P, T, D])
        x2T = sb("x2T", [P, N])
        x2T_hi, x2T_lo = sb("x2T_hi", [P, N], F32R), sb("x2T_lo", [P, N], F32R)
        c1 = sb("c1", [P, N])
        c1_hi = sb("c1_hi", [P, N + 2 * PAD], F32R)
        c1_lo = sb("c1_lo", [P, N + 2 * PAD], F32R)
        dist_l = sb("dist_l", [P, N])
        dist_r = sb("dist_r", [P, N])
        msg_pre = sb("msg_pre", [P, T, D])
        msg = sb("msg", [P, T, D])
        near = sb("near", [P, T * N])
        nearT = sb("nearT", [P, T * N])
        conv_sum = sb("conv_sum", [P, N])
        convT = sb("convT", [P, N])
        convT_hi, convT_lo = sb("convT_hi", [P, N], F32R), sb("convT_lo", [P, N], F32R)
        nmpT_hi, nmpT_lo = sb("nmpT_hi", [P, N], F32R), sb("nmpT_lo", [P, N], F32R)
        r_tanh = sb("r_tanh", [P, N])
        z_tanh = sb("z_tanh", [P, N])
        hn_half = sb("hn_half", [P, N])
        r_hn = sb("r_hn", [P, N])
        n_pre = sb("n_pre", [P, N])
        nT = sb("nT", [P, N])
        x_less_n = sb("x_less_n", [P, N])
        z_part = sb("z_part", [P, N])
        n_plus_x = sb("n_plus_x", [P, N])
        y2T = sb("y2T", [P, N])
        x3 = sb("x3", [P, 2, T, D])
        x3T = sb("x3T", [P, N])
        x3T_hi, x3T_lo = sb("x3T_hi", [P, N], F32R), sb("x3T_lo", [P, N], F32R)
        q_hilo = sb("q_hilo", [P, 2, N], F32R)
        q_shift = sb("q_shift", [P, 2, N], F32R)
        k_hi = sb("k_hi", [P, 2, N], F32R)
        k_lo = sb("k_lo", [P, 2, N], F32R)
        kh_head = sb("kh_head", [P, HEADS, N], F32R)
        kl_head = sb("kl_head", [P, HEADS, N], F32R)
        v_one = sb("v_one", [P, T, HEADS, 32])
        maxima = sb("maxima", [P, T, P])
        weights = sb("weights", [P, 3, T * N])
        oT = sb("oT", [P, 2, N])
        inv_sum = sb("inv_sum", [P, T * HEADS])
        o = sb("o", [P, T, D])
        oT_all = sb("oT_all", [P, N])
        result = sb("result", [P, T, D])

        la, lb, lc = (ctx.enter_context(nc.psum_tensor(f"layer_bank{i}", [P, 512], F32)) for i in range(3))
        score = ctx.enter_context(nc.psum_tensor("score_banks", [P, 4, 512], F32))
        att = ctx.enter_context(nc.psum_tensor("att_bank", [P, 512], F32))

        products = """
            const_loaded conv2_loaded w_hi conv2_hi we_ident setup_dve setup_pool setup_chain pool_chain pool_passed sp_passed dve_passed
            loaded adjT_att stored
            deg deg_eps norm x_less1 proj0 hom_in gate_het gate_tanh agg0 hom_het gated mixed mixed_exp relu_part
            x1 x1_pT x1T agg1 hT hid_p hidT out1_p x1_b2
            x2 x2_pT x2T_hi x2T x2T_lo conv1_p c1_hi c1 c1_lo se_p dist_dve dist_act msg_p msg_pre msg dist_p near nearT
            conv2_p conv_sum convT_hi convT convT_lo nmp_p nmpT_hi nmpT_lo r_p z_p r_tanh z_tanh gn_p hn_half r_hn n_pre nT x_less_n z_part n_plus_x
            y2T y2_p x3 x3_pT x3T_hi x3T x3T_lo
            q_p q_hi q_lo q_copy k_p k_hi k_lo kh_head kl_head v_p v_one masks s1_p maxima max_pT shift
            s2_p biased weight pv oT o_p inv_sum o o_pT oT_all wo_p result
        """.split()
        ready = {name: sem(f"{name}_ready") for name in products}
        y_ready = [sem(f"y{k}_ready") for k in range(4)]
        stats_ready = [sem(f"stats{k}_ready") for k in range(4)]
        moments_ready = [sem(f"moments{k}_ready") for k in range(4)]
        var_eps_ready = [sem(f"var_eps{k}_ready") for k in range(4)]
        rstd_ready = [sem(f"rstd{k}_ready") for k in range(4)]
        block = ctx.enter_context(nc.Block())

        def wait(eng, semaphore, count):
            if not isinstance(count, int) or count > 0:
                eng.wait_ge(semaphore, count)

        def count(eng, value):
            return value if isinstance(value, int) else eng.snap(value)

        def first_step(body):
            body(-1, 1, True, False, False, False)

        def steps(eng, body):
            body(0, 0, True, True, False, False)
            body(1, 1, True, True, True, False)
            with eng.Fori(0, BATCH // 2 - 2) as i:
                for half in (0, 1):
                    body(i * 2 + (2 + half), half, True, True, True, True)
            body(BATCH - 2, 0, True, True, True, True)
            body(BATCH - 1, 1, False, True, True, True)
            body(BATCH, 0, False, False, True, True)
            body(BATCH + 1, 1, False, False, False, True)

        @block.sync
        def _(sp):
            def load(graph, buf):
                at = bass.ds(graph, 1)
                sp.dma_start(x_in[:, buf], x[at].rearrange("o (t p) d -> p (o t) d", p=P)).then_inc(ready["loaded"], 16)
                sp.dma_start(xT_in[:, buf], xT[at].rearrange("o d n -> d (o n)")).then_inc(ready["loaded"], 16)
                sp.dma_start(adj_in[:, buf], adj[at].rearrange("o (t p) m -> p (o t) m", p=P)).then_inc(ready["loaded"], 16)
                sp.dma_start(adjT_in[:, buf], adjT[at].rearrange("o (t p) n -> p (o t) n", p=P)).then_inc(ready["loaded"], 16)

            def body(s, buf, finish, more):
                if finish:
                    sp.wait_ge(ready["result"], count(sp, s * 2 - 2))
                    sp.nop().then_inc(ready["sp_passed"], 1)
                    sp.dma_start(out[bass.ds(s - 2, 1)].rearrange("o (t p) d -> p (o t) d", p=P), result[:]).then_inc(ready["stored"], 16)
                if more:
                    sp.wait_ge(ready["loaded"], count(sp, (s + 2) * 64))
                    sp.nop().then_inc(ready["sp_passed"], 1)
                    sp.wait_ge(ready["masks"], count(sp, (s + 1) * 3))
                    sp.nop().then_inc(ready["sp_passed"], 1)
                    sp.wait_ge(ready["nearT"], count(sp, s + 1))
                    sp.nop().then_inc(ready["sp_passed"], 1)
                    load(s + 2, buf)
                if not isinstance(s, int) or 0 < s < BATCH:
                    sp.wait_ge(ready["biased"], count(sp, s * HEADS))
                    sp.nop().then_inc(ready["sp_passed"], 1)
                if not isinstance(s, int) or s < BATCH:
                    sp.dma_start(adjT_att[:].rearrange("p (t n) -> p t n", t=T),
                                 adjT[bass.ds(s, 1)].rearrange("o (t p) n -> p (o t) n", p=P)).then_inc(ready["adjT_att"], 16)

            sp.nop().then_inc(ready["stored"], 16)
            sp.dma_start(consts[:], packed).then_inc(ready["const_loaded"], 16)
            load(0, 0)
            sp.dma_start(conv2_w[:], conv2).then_inc(ready["conv2_loaded"], 16)
            sp.wait_ge(ready["loaded"], 64)
            load(1, 1)
            body(0, 0, False, True)
            body(1, 1, False, True)
            with sp.Fori(0, BATCH // 2 - 2) as i:
                for half in (0, 1):
                    body(i * 2 + (2 + half), half, True, True)
            for s in range(BATCH - 2, BATCH + 2):
                body(s, s % 2, True, False)
            sp.wait_ge(ready["stored"], 16 * (BATCH + 1))

        @block.gpsimd
        def _(pool):
            links = [0]

            def link(instruction):
                links[0] += 1
                instruction.then_inc(ready["pool_chain"], 1)
                pool.wait_ge(ready["pool_chain"], links[0])

            link(pool.memset(minus_half[:], -0.5))
            pool.wait_ge(ready["const_loaded"], 16)
            for k, bn in enumerate(("bn1", "bn2")):
                link(pool.tensor_scalar(bn_mean[:, k:k + 1], const(bn, 3, 1), EPS, None, ALU.add))
                pool.tensor_tensor(bn_rstd[:, k:k + 1], bn_mean[:, k:k + 1], minus_half[:, 0:1], ALU.pow).then_inc(ready["setup_pool"], 1)

            def layer_norm(k, n, n2):
                pool.wait_ge(moments_ready[k], n2)
                pool.nop().then_inc(ready["pool_passed"], 1)
                pool.tensor_scalar(var_eps[k][:], moments[k][:, :, 1], EPS, None, ALU.add).then_inc(var_eps_ready[k], 1)
                pool.wait_ge(var_eps_ready[k], n)
                pool.tensor_tensor(rstd[k][:], var_eps[k][:], minus_half[:], ALU.pow).then_inc(rstd_ready[k], 1)

            def body(s, buf, front, layers, attention, finish):
                f, n, m, e = count(pool, s + 2), count(pool, s + 1), count(pool, s), count(pool, s - 1)
                f2, n2, m2, e2 = count(pool, s * 2 + 4), count(pool, s * 2 + 2), count(pool, s * 2), count(pool, s * 2 - 2)
                if layers:
                    pool.wait_ge(ready["x1"], n2)
                    pool.tensor_tensor(x1_b2[:], x1[:], const("b2_row").rearrange("p (o d) -> p o d", o=1).broadcast_to([P, T, D]),
                                       ALU.add).then_inc(ready["x1_b2"], 1)
                if front:
                    pool.wait_ge(ready["deg"], f)
                    pool.nop().then_inc(ready["pool_passed"], 1)
                    pool.tensor_scalar(deg_eps[:], deg[:], 1e-6, None, ALU.add).then_inc(ready["deg_eps"], 1)
                    pool.wait_ge(ready["deg_eps"], f)
                    pool.tensor_tensor(norm[:], deg_eps[:], minus_half[:], ALU.pow).then_inc(ready["norm"], 1)
                if attention:
                    layer_norm(2, m, m2)
                if layers:
                    layer_norm(1, n, n2)
                if finish:
                    layer_norm(3, e, e2)
                if front:
                    layer_norm(0, f, f2)
                if layers:
                    pool.wait_ge(ready["nT"], n)
                    pool.tensor_tensor(n_plus_x[:], nT[:], x2T[:], ALU.add).then_inc(ready["n_plus_x"], 1)

            first_step(body)
            steps(pool, body)

        @block.scalar
        def _(act):
            act.wait_ge(ready["const_loaded"], 16)
            act.activation(w_hi[:], consts[:, 0:SPLIT], ACT.Copy).then_inc(ready["w_hi"], 1)

            def body(s, buf, front, layers, attention, finish):
                f, n, m, e = count(act, s + 2), count(act, s + 1), count(act, s), count(act, s - 1)

                def high_of_head(h):
                    act.activation(kh_head[:, h], k_hi[:, h // GH].bitcast(F32), ACT.Copy,
                                   scale=const("head_rows", h % GH, 1)).then_inc(ready["kh_head"], 1)

                def exponentials(h, step=s):
                    act.wait_ge(ready["biased"], step * HEADS - (HEADS - 1 - h))
                    act.activation(weights[:, h % 3], weights[:, h % 3], ACT.Exp).then_inc(ready["weight"], 1)

                if layers:
                    act.wait_ge(ready["x1_pT"], n)
                    act.activation(x1T[:], la[:, 0:N], ACT.Copy).then_inc(ready["x1T"], 1)
                if finish:
                    exponentials(6, s - 1)
                if layers:
                    act.wait_ge(ready["hid_p"], n)
                    for k in range(2):
                        act.activation(hidT[:, k], lc[:, k * N:(k + 1) * N], ACT.Relu, bias=const("b1", k, 1)).then_inc(ready["hidT"], 1)
                if front:
                    act.wait_ge(ready["norm"], f)
                    act.wait_ge(ready["proj0"], s * 2 + 3)
                    act.activation(hom_in[:, 0], la[:, 0:D], ACT.Copy, scale=norm[:, 0:1]).then_inc(ready["hom_in"], 1)
                if finish:
                    exponentials(7, s - 1)
                    act.wait_ge(ready["pv"], s * HEADS - HEADS)
                    act.activation(oT[:], att[:].rearrange("p (g n) -> p g n", g=2), ACT.Copy).then_inc(ready["oT"], 1)
                if attention:
                    act.wait_ge(ready["x3_pT"], m)
                    act.activation(x3T[:], score[:, 0, 0:N], ACT.Copy).then_inc(ready["x3T"], 1)
                    act.activation(x3T_hi[:], score[:, 0, 0:N], ACT.Copy).then_inc(ready["x3T_hi"], 1)
                    act.wait_ge(ready["v_p"], m)
                    act.activation(v_one[:, :, :, 0:HD], att[:, 0:N].rearrange("p (t h d) -> p t h d", t=T, h=HEADS), ACT.Copy).then_inc(ready["v_one"], 1)
                if front:
                    act.wait_ge(ready["proj0"], s * 2 + 4)
                    act.activation(hom_in[:, 1], lc[:, 0:D], ACT.Copy, scale=norm[:, 1:2]).then_inc(ready["hom_in"], 1)
                if attention:
                    act.wait_ge(ready["q_p"], m)
                    act.activation(q_hilo[:], score[:, 0].rearrange("p (g n) -> p g n", g=2), ACT.Copy, scale=HD ** -0.5).then_inc(ready["q_hi"], 1)
                    act.wait_ge(ready["k_p"], m)
                    act.activation(k_hi[:], score[:, 1].rearrange("p (g n) -> p g n", g=2), ACT.Copy).then_inc(ready["k_hi"], 1)
                if finish:
                    act.wait_ge(ready["o_pT"], e)
                    act.activation(oT_all[:], score[:, 2, 0:N], ACT.Copy).then_inc(ready["oT_all"], 1)
                if layers:
                    act.wait_ge(ready["x2_pT"], n)
                    act.activation(x2T_hi[:], la[:, 0:N], ACT.Copy).then_inc(ready["x2T_hi"], 1)
                    act.activation(x2T[:], la[:, 0:N], ACT.Copy).then_inc(ready["x2T"], 1)
                if attention:
                    act.wait_ge(ready["k_hi"], m)
                    high_of_head(0)
                    high_of_head(1)
                    high_of_head(2)
                    high_of_head(3)
                    act.activation(q_shift[0:HALF], q_hilo[0:HALF].bitcast(F32), ACT.Copy).then_inc(ready["q_copy"], 1)
                if layers:
                    act.activation(adj_round[:, buf], adj_in[:, buf].rearrange("p t m -> p (t m)"), ACT.Copy).then_inc(ready["masks"], 1)
                    act.wait_ge(ready["conv1_p"], n)
                    for dst, name in ((c1_hi[:, PAD:PAD + N], "c1_hi"), (c1[:], "c1")):
                        act.activation(dst, lb[:, 0:N], ACT.Relu, bias=bn_bias[:, 0:1], scale=bn_scale[:, 0:1]).then_inc(ready[name], 1)
                    act.wait_ge(ready["se_p"], n)
                    act.activation(dist_r[32:64], lc[32:64, 0:N], ACT.Square, bias=const("bse")[32:64]).then_inc(ready["dist_act"], 1)
                if front:
                    wait(act, ready["relu_part"], n)
                    act.wait_ge(ready["loaded"], s * 64 + 128)
                    act.activation(x_less1[:], x_in[:, 1 - buf], ACT.Copy, bias=-1.0).then_inc(ready["x_less1"], 1)
                if layers:
                    act.activation(dist_l[64:96], lc[64:96, 0:N], ACT.Square, bias=const("bse")[64:96]).then_inc(ready["dist_act"], 1)
                if front:
                    act.wait_ge(ready["gate_het"], s * 2 + 4)
                    act.activation(gate_tanh[:], gate_het[:, :, D:2 * D], ACT.Tanh, scale=0.5).then_inc(ready["gate_tanh"], 1)
                if attention:
                    for h in range(4, HEADS):
                        high_of_head(h)
                if layers:
                    act.wait_ge(ready["dist_p"], n)
                    act.activation(near[:], lc[:], ACT.Exp, scale=2.0).then_inc(ready["near"], 1)
                if front:
                    act.wait_ge(ready["mixed"], f)
                    act.activation(mixed_exp[:], mixed[:], ACT.Exp).then_inc(ready["mixed_exp"], 1)
                if attention:
                    act.wait_ge(ready["max_pT"], m)
                    for g in range(2):
                        act.activation(q_shift[HALF:HALF + 32, g], att[HALF:HALF + 32, 0:N], ACT.Copy, scale=-1.0).then_inc(ready["shift"], 1)
                if layers:
                    act.wait_ge(ready["msg_pre"], n)
                    act.activation(msg[:], msg_pre[:], ACT.Relu).then_inc(ready["msg"], 1)
                    act.wait_ge(ready["conv_sum"], s + 1)
                    act.activation(convT[:], conv_sum[:], ACT.Relu, bias=bn_bias[:, 1:2]).then_inc(ready["convT"], 1)
                    act.wait_ge(ready["conv_sum"], n)
                    act.activation(convT_hi[:], conv_sum[:], ACT.Relu, bias=bn_bias[:, 1:2]).then_inc(ready["convT_hi"], 1)
                    act.wait_ge(ready["nmp_p"], n)
                    act.activation(nmpT_hi[:], la[:, 0:N], ACT.Copy).then_inc(ready["nmpT_hi"], 1)
                if attention:
                    exponentials(0)
                    exponentials(1)
                    exponentials(2)
                if layers:
                    act.wait_ge(ready["r_p"], n)
                    act.activation(r_tanh[:], lc[:, 0:N], ACT.Tanh, bias=gate_bias[:, 0:1], scale=0.5).then_inc(ready["r_tanh"], 1)
                if attention:
                    exponentials(3)
                    exponentials(4)
                if layers:
                    act.wait_ge(ready["n_pre"], n)
                    act.activation(nT[:], n_pre[:], ACT.Tanh, bias=const("bih", 2, 1)).then_inc(ready["nT"], 1)
                    act.wait_ge(ready["z_p"], n)
                    act.activation(z_tanh[:], la[:, 0:N], ACT.Tanh, bias=gate_bias[:, 1:2], scale=0.5).then_inc(ready["z_tanh"], 1)
                if attention:
                    exponentials(5)

            first_step(body)
            act.wait_ge(ready["conv2_loaded"], 16)
            act.activation(conv2_hi[:], conv2_w[:], ACT.Copy).then_inc(ready["conv2_hi"], 1)
            for h in range(HEADS):
                act.activation(we_ident[:, h], const("ident"), ACT.Copy, scale=const("we", h, 1)).then_inc(ready["we_ident"], 1)
            act.wait_ge(ready["setup_dve"], 1)
            steps(act, body)

        @block.vector
        def _(dve):
            links = [0]

            def link(instruction):
                links[0] += 1
                instruction.then_inc(ready["setup_chain"], 1)
                dve.wait_ge(ready["setup_chain"], links[0])

            def free(instruction):
                links[0] += 1
                instruction.then_inc(ready["setup_chain"], 1)

            free(dve.memset(c1_hi[:].bitcast(F32), 0.0))
            free(dve.memset(c1_lo[:].bitcast(F32), 0.0))
            free(dve.memset(maxima[:], 0.0))
            free(dve.memset(q_shift[:].bitcast(F32), 0.0))
            free(dve.memset(kl_head[:].bitcast(F32), 0.0))
            link(dve.memset(v_one[:], 0.0))
            free(dve.memset(v_one[:, :, :, HD:HD + 1], 1.0))
            free(dve.memset(dist_l[32:64], -0.5))
            free(dve.memset(dist_r[64:96], -0.5))
            dve.wait_ge(ready["const_loaded"], 16)
            link(dve.tensor_scalar(one_eps[:], const("eps"), 1.0, None, ALU.add))

            def second_setup():
                for h in range(HEADS):
                    free(dve.tensor_scalar(kl_head[HALF:P, h], kl_head[HALF:P, h].bitcast(F32), const("shift_rows", h, 1)[HALF:P], None, ALU.add))
                free(dve.tensor_copy(ident16[:], const("ident")))
                dve.wait_ge(ready["setup_pool"], 2)
                for k, bn in enumerate(("bn1", "bn2")):
                    link(dve.tensor_tensor(bn_scale[:, k:k + 1], bn_rstd[:, k:k + 1], const(bn, 0, 1), ALU.mult))
                    link(dve.tensor_tensor(bn_mean[:, k:k + 1], const(bn, 2, 1), bn_scale[:, k:k + 1], ALU.mult))
                    free(dve.tensor_tensor(bn_bias[:, k:k + 1], const(bn, 1, 1), bn_mean[:, k:k + 1], ALU.subtract))
                link(dve.tensor_tensor(gate_sum[:], const("bih", 0, 2), const("bhh", 0, 2), ALU.add))
                free(dve.tensor_scalar(gate_bias[:], gate_sum[:], 0.5, None, ALU.mult))
                dve.wait_ge(ready["w_hi"], 1)
                free(dve.tensor_tensor(w_lo[:], consts[:, 0:SPLIT], w_hi[:].bitcast(F32), ALU.subtract))
                dve.wait_ge(ready["conv2_hi"], 1)
                link(dve.tensor_tensor(conv2_lo[:], conv2_w[:], conv2_hi[:].bitcast(F32), ALU.subtract))
                dve.nop().then_inc(ready["setup_dve"], 1)

            def moments_of(k, n2, src):
                for t in range(T):
                    dve.bn_stats(stats[k][:, t], src(t)).then_inc(stats_ready[k], 1)
                dve.wait_ge(stats_ready[k], n2)
                dve.nop().then_inc(ready["dve_passed"], 1)
                for t in range(T):
                    dve.bn_aggr(moments[k][:, t], stats[k][:, t]).then_inc(moments_ready[k], 1)

            def normalise(k, n, n2, dst, src, name):
                dve.wait_ge(moments_ready[k], n2)
                dve.wait_ge(rstd_ready[k], n)
                for t in range(T):
                    dve.tensor_scalar(dst[:, t], src(t), moments[k][:, t, 0:1], rstd[k][:, t:t + 1],
                                      ALU.subtract, ALU.mult).then_inc(ready[name], 1)

            def body(s, buf, front, layers, attention, finish):
                f, n, m, e = count(dve, s + 2), count(dve, s + 1), count(dve, s), count(dve, s - 1)
                f2, n2, m2, e2 = count(dve, s * 2 + 4), count(dve, s * 2 + 2), count(dve, s * 2), count(dve, s * 2 - 2)
                heads = [s * HEADS - (HEADS - 1 - h) for h in range(HEADS)]

                def maximum(pair):
                    dve.wait_ge(ready["s1_p"], s * 4 - (3 - pair))
                    banks = score[:, 2 * (pair % 2):2 * (pair % 2) + 2].rearrange("p h (t j) -> p h t j", t=T)
                    dst = maxima[:, :, HALF + 2 * pair:HALF + 2 * pair + 2].rearrange("p t h -> p h t")
                    dve.tensor_reduce(dst, banks, AX_X, ALU.max).then_inc(ready["maxima"], 1)

                def low_of_head(h):
                    dve.tensor_scalar(kl_head[0:HALF, h], k_lo[0:HALF, h // GH].bitcast(F32),
                                      const("head_rows", h % GH, 1)[0:HALF], None, ALU.mult).then_inc(ready["kl_head"], 1)

                def bias(h, step=s):
                    dve.wait_ge(ready["adjT_att"], step * 16)
                    dve.wait_ge(ready["s2_p"], step * HEADS - (HEADS - 1 - h))
                    if h >= 3:
                        dve.wait_ge(ready["pv"], step * HEADS - (HEADS - 1 - (h - 3)))
                    dve.scalar_tensor_tensor(out=weights[:, h % 3], in0=adjT_att[:], scalar=const("we", h, 1), in1=score[:, h % 4],
                                             op0=ALU.mult, op1=ALU.add).then_inc(ready["biased"], 1)

                def gate_and_het(t, bank):
                    dve.wait_ge(ready["hom_in"], s * 2 + 3 + t)
                    dve.tensor_tensor(gate_het[:, t], bank[:, D:3 * D], const("het_bt_row"), ALU.add).then_inc(ready["gate_het"], 1)

                if front:
                    dve.wait_ge(ready["loaded"], s * 64 + 128)
                    dve.tensor_reduce(deg[:], adj_in[:, 1 - buf], AX_X, ALU.add).then_inc(ready["deg"], 1)
                if layers:
                    dve.wait_ge(ready["agg1"], n)
                    dve.wait_ge(ready["x1T"], n)
                    dve.scalar_tensor_tensor(out=hT[:], in0=x1T[:], scalar=one_eps[:], in1=lb[:, 0:N], op0=ALU.mult,
                                             op1=ALU.add).then_inc(ready["hT"], 1)
                if attention:
                    dve.wait_ge(ready["y2_p"], m)
                    moments_of(2, m2, lambda t: score[:, 0, t * D:(t + 1) * D])
                if finish:
                    bias(7, s - 1)
                if attention:
                    normalise(2, m, m2, x3[:, 1 - buf], lambda t: score[:, 0, t * D:(t + 1) * D], "x3")
                if front:
                    gate_and_het(0, la)
                if layers:
                    dve.wait_ge(ready["out1_p"], n)
                    dve.wait_ge(ready["x1_b2"], n)
                    dve.tensor_tensor(y[1][:], lb[:, 0:N].rearrange("p (t d) -> p t d", t=T), x1_b2[:], ALU.add).then_inc(y_ready[1], 1)
                    dve.wait_ge(y_ready[1], n)
                    moments_of(1, n2, lambda t: y[1][:, t])
                if attention:
                    dve.wait_ge(ready["x3T"], m)
                    dve.wait_ge(ready["x3T_hi"], m)
                    dve.tensor_tensor(x3T_lo[:], x3T[:], x3T_hi[:].bitcast(F32), ALU.subtract).then_inc(ready["x3T_lo"], 1)
                if finish:
                    dve.wait_ge(ready["o_p"], e)
                    by_head = score[:, 1].rearrange("p (a c) -> p a c", c=32)
                    dve.reciprocal(inv_sum[:].rearrange("p (a o) -> p a o", o=1), by_head[:, :, HD:HD + 1]).then_inc(ready["inv_sum"], 1)
                    dve.wait_ge(ready["inv_sum"], e)
                    dve.tensor_tensor(o[:].rearrange("p t (h d) -> p (t h) d", d=HD), by_head[:, :, 0:HD],
                                      inv_sum[:].rearrange("p (a o) -> p a o", o=1).broadcast_to([P, T * HEADS, HD]), ALU.mult
                                      ).then_inc(ready["o"], 1)
                if layers:
                    normalise(1, n, n2, x2, lambda t: y[1][:, t], "x2")
                if attention:
                    dve.wait_ge(ready["q_hi"], m)
                    dve.scalar_tensor_tensor(out=q_hilo[HALF:P], in0=score[HALF:P, 0].rearrange("p (g n) -> p g n", g=2), scalar=HD ** -0.5,
                                             in1=q_hilo[HALF:P].bitcast(F32), op0=ALU.mult, op1=ALU.subtract).then_inc(ready["q_lo"], 1)
                    dve.wait_ge(ready["k_hi"], m)
                    dve.tensor_tensor(k_lo[0:HALF], score[0:HALF, 1].rearrange("p (g n) -> p g n", g=2), k_hi[0:HALF].bitcast(F32),
                                      ALU.subtract).then_inc(ready["k_lo"], 1)
                if front:
                    gate_and_het(1, lc)
                if finish:
                    dve.wait_ge(ready["wo_p"], e)
                    dve.tensor_tensor(y[3][:], score[:, 2, N:2 * N].rearrange("p (t d) -> p t d", t=T), x3[:, buf], ALU.add).then_inc(y_ready[3], 1)
                if layers:
                    dve.wait_ge(ready["x2T"], n)
                    dve.wait_ge(ready["x2T_hi"], n)
                    dve.tensor_tensor(x2T_lo[:], x2T[:], x2T_hi[:].bitcast(F32), ALU.subtract).then_inc(ready["x2T_lo"], 1)
                if finish:
                    dve.wait_ge(y_ready[3], e)
                    moments_of(3, e2, lambda t: y[3][:, t])
                if front:
                    dve.wait_ge(ready["agg0"], f)
                    dve.wait_ge(ready["gate_het"], f2)
                    for t in range(T):
                        dve.scalar_tensor_tensor(out=hom_het[:, t], in0=att[:, t * D:(t + 1) * D], scalar=norm[:, t:t + 1], in1=gate_het[:, t, 0:D],
                                                 op0=ALU.mult, op1=ALU.subtract).then_inc(ready["hom_het"], 1)
                if attention:
                    maximum(0)
                    maximum(1)
                if layers:
                    dve.tensor_scalar(mask[:, buf], adj_in[:, buf].rearrange("p t m -> p (t m)"), 0.0, MASKED,
                                      ALU.is_equal, ALU.mult).then_inc(ready["masks"], 1)
                    dve.wait_ge(ready["msg_p"], n)
                    dve.tensor_tensor(msg_pre[:], la[:, 0:N].rearrange("p (t d) -> p t d", t=T),
                                      const("bmsg_row").rearrange("p (o d) -> p o d", o=1).broadcast_to([P, T, D]), ALU.add
                                      ).then_inc(ready["msg_pre"], 1)
                    dve.wait_ge(ready["se_p"], n)
                    for dst in (dist_l, dist_r):
                        dve.tensor_scalar(dst[0:32], lc[0:32, 0:N], const("bse")[0:32], None, ALU.add).then_inc(ready["dist_dve"], 1)
                    dve.wait_ge(ready["c1"], n)
                    dve.wait_ge(ready["c1_hi"], n)
                    dve.tensor_tensor(c1_lo[:, PAD:PAD + N], c1[:], c1_hi[:, PAD:PAD + N].bitcast(F32), ALU.subtract).then_inc(ready["c1_lo"], 1)
                    dve.tensor_scalar(maskT[:, buf], adjT_in[:, buf].rearrange("p t m -> p (t m)"), 0.0, MASKED,
                                      ALU.is_equal, ALU.mult).then_inc(ready["masks"], 1)
                if attention:
                    maximum(2)
                if front:
                    dve.wait_ge(ready["hom_het"], f2)
                    dve.wait_ge(ready["gate_tanh"], f)
                    dve.scalar_tensor_tensor(out=gated[:], in0=gate_tanh[:], scalar=1.0, in1=hom_het[:], op0=ALU.add,
                                             op1=ALU.mult).then_inc(ready["gated"], 1)
                    dve.wait_ge(ready["gated"], f)
                    dve.scalar_tensor_tensor(out=mixed[:], in0=gated[:], scalar=0.5, in1=gate_het[:, :, 0:D], op0=ALU.mult,
                                             op1=ALU.add).then_inc(ready["mixed"], 1)
                if attention:
                    maximum(3)
                    dve.wait_ge(ready["k_lo"], m)
                    for h in range(0, 4):
                        low_of_head(h)
                if front:
                    dve.wait_ge(ready["mixed"], f)
                    dve.wait_ge(ready["x_less1"], f)
                    dve.scalar_tensor_tensor(out=relu_part[:], in0=mixed[:], scalar=0.0, in1=x_less1[:], op0=ALU.max,
                                             op1=ALU.add).then_inc(ready["relu_part"], 1)
                    dve.wait_ge(ready["relu_part"], f)
                    dve.wait_ge(ready["mixed_exp"], f)
                    dve.scalar_tensor_tensor(out=y[0][:], in0=mixed_exp[:], scalar=1.0, in1=relu_part[:], op0=ALU.min,
                                             op1=ALU.add).then_inc(y_ready[0], 1)
                if layers:
                    dve.wait_ge(ready["near"], n)
                    dve.tensor_tensor(nearT[:], near[:], adjT_in[:, buf].rearrange("p t n -> p (t n)"), ALU.mult).then_inc(ready["nearT"], 1)
                if attention:
                    for h in range(4, HEADS):
                        low_of_head(h)
                    bias(0)
                if layers:
                    dve.wait_ge(ready["conv2_p"], n)
                    dve.scalar_tensor_tensor(out=conv_sum[:], in0=lb[:, 0:N], scalar=bn_scale[:, 1:2], in1=x2T[:], op0=ALU.mult,
                                             op1=ALU.add).then_inc(ready["conv_sum"], 1)
                if attention:
                    bias(1)
                if front:
                    dve.wait_ge(y_ready[0], f)
                    moments_of(0, f2, lambda t: y[0][:, t])
                if layers:
                    dve.wait_ge(ready["convT"], n)
                    dve.wait_ge(ready["convT_hi"], n)
                    dve.tensor_tensor(convT_lo[:], convT[:], convT_hi[:].bitcast(F32), ALU.subtract).then_inc(ready["convT_lo"], 1)
                    dve.wait_ge(ready["nmpT_hi"], n)
                    dve.tensor_tensor(nmpT_lo[:], la[:, 0:N], nmpT_hi[:].bitcast(F32), ALU.subtract).then_inc(ready["nmpT_lo"], 1)
                if attention:
                    bias(2)
                if finish:
                    dve.wait_ge(ready["stored"], s * 16 - 16)
                    normalise(3, e, e2, result, lambda t: y[3][:, t], "result")
                if front:
                    normalise(0, f, f2, x1, lambda t: y[0][:, t], "x1")
                if attention:
                    bias(3)
                if layers:
                    dve.wait_ge(ready["gn_p"], n)
                    dve.tensor_scalar(hn_half[:], lb[:, N:2 * N], const("bhh", 2, 1), 0.5, ALU.add, ALU.mult).then_inc(ready["hn_half"], 1)
                if attention:
                    bias(4)
                if layers:
                    dve.wait_ge(ready["hn_half"], n)
                    dve.wait_ge(ready["r_tanh"], n)
                    dve.scalar_tensor_tensor(out=r_hn[:], in0=r_tanh[:], scalar=1.0, in1=hn_half[:], op0=ALU.add,
                                             op1=ALU.mult).then_inc(ready["r_hn"], 1)
                    dve.wait_ge(ready["r_hn"], n)
                    dve.tensor_tensor(n_pre[:], lb[:, 0:N], r_hn[:], ALU.add).then_inc(ready["n_pre"], 1)
                if attention:
                    bias(5)
                if layers:
                    dve.wait_ge(ready["nT"], n)
                    dve.tensor_tensor(x_less_n[:], x2T[:], nT[:], ALU.subtract).then_inc(ready["x_less_n"], 1)
                    dve.wait_ge(ready["x_less_n"], n)
                    dve.wait_ge(ready["z_tanh"], n)
                    dve.scalar_tensor_tensor(out=z_part[:], in0=z_tanh[:], scalar=1.0, in1=x_less_n[:], op0=ALU.add,
                                             op1=ALU.mult).then_inc(ready["z_part"], 1)
                    dve.wait_ge(ready["z_part"], n)
                    dve.wait_ge(ready["n_plus_x"], n)
                    dve.scalar_tensor_tensor(out=y2T[:], in0=z_part[:], scalar=0.5, in1=n_plus_x[:], op0=ALU.mult,
                                             op1=ALU.add).then_inc(ready["y2T"], 1)
                if attention:
                    bias(6)

            first_step(body)
            second_setup()
            steps(dve, body)

        @block.tensor
        def _(pe):
            pe.wait_ge(ready["const_loaded"], 16)

            def turn(dst, src, name):
                for t in range(T):
                    last = pe.transpose(dst[:, t * P:(t + 1) * P], src(t), const("ident"))
                last.then_inc(ready[name], 1)

            def body(s, buf, front, layers, attention, finish):
                f, n, m, e = count(pe, s + 2), count(pe, s + 1), count(pe, s), count(pe, s - 1)
                n2 = count(pe, s * 2 + 2)
                heads = [s * HEADS - (HEADS - 1 - h) for h in range(HEADS)]

                def scores_for_maxima(pair):
                    for h in (2 * pair, 2 * pair + 1):
                        bank = score[:, h % 4]
                        pe.matmul(bank, ident16[:], mask[:, 1 - buf], start=True, stop=False)
                        pe.matmul(bank, we_ident[:, h], adj_round[:, 1 - buf], start=False, stop=False)
                        pe.wait_ge(ready["kh_head"], heads[h])
                        for t in range(T):
                            last = pe.matmul(bank[:, t * N:(t + 1) * N], q_hilo[:, h // GH, t * P:(t + 1) * P], kh_head[:, h],
                                             start=False, stop=t == T - 1)
                    last.then_inc(ready["s1_p"], 1)

                def scores(h, step=s, graph_buf=1 - buf):
                    if h >= 4:
                        pe.wait_ge(ready["biased"], step * HEADS - (HEADS - 1 - (h - 4)))
                    bank = score[:, h % 4]
                    pe.matmul(bank, ident16[:], maskT[:, graph_buf], start=True, stop=False)
                    pe.wait_ge(ready["kl_head"], step * HEADS - (HEADS - 1 - h))
                    for t in range(T):
                        cols = bank[:, t * N:(t + 1) * N]
                        pe.matmul(cols, kh_head[:, h, t * P:(t + 1) * P], q_hilo[:, h // GH], start=False, stop=False)
                        last = pe.matmul(cols, kl_head[:, h, t * P:(t + 1) * P], q_shift[:, h // GH], start=False, stop=t == T - 1)
                    last.then_inc(ready["s2_p"], 1)

                def weigh(h, step=s):
                    pe.wait_ge(ready["weight"], step * HEADS - (HEADS - 1 - h))
                    rows = 32 * (h % GH)
                    for t in range(T):
                        last = pe.matmul(att[rows:rows + 32, (h // GH) * N:(h // GH + 1) * N], v_one[:, t, h],
                                         weights[:, h % 3, t * N:(t + 1) * N], start=t == 0, stop=t == T - 1)
                    last.then_inc(ready["pv"], 1)

                def project(t, bank):
                    pe.matmul(bank[:, 0:3 * D], xT_in[:, 1 - buf, t * P:(t + 1) * P], const("w0"), start=True, stop=True
                              ).then_inc(ready["proj0"], 1)

                def conv2_pass(w, c, first=False, final=False):
                    for k in range(TAPS):
                        last = pe.matmul(lb[:, 0:N], w[:, k * D:(k + 1) * D], c[:, k:k + N],
                                         start=first and k == 0, stop=final and k == TAPS - 1)
                    if final:
                        last.then_inc(ready["conv2_p"], 1)

                def project_heads(dst, w, name):
                    for g in range(2):
                        last = product(pe, dst[:, g * N:(g + 1) * N], w, g * P, (x3T_hi, x3T_lo))
                    last.then_inc(ready[name], 1)

                if layers:
                    pe.wait_ge(ready["x1"], n2)
                    if attention:
                        pe.wait_ge(ready["z_tanh"], m)
                        pe.wait_ge(ready["n_pre"], m)
                    turn(la, lambda t: x1[:, t], "x1_pT")
                    for k in range(T):
                        last = pe.matmul(lb[:, 0:N], x1[:, k], adjT_in[:, buf, k], start=k == 0, stop=k == T - 1)
                    last.then_inc(ready["agg1"], 1)
                if attention:
                    pe.wait_ge(ready["y2T"], m)
                    if finish:
                        pe.wait_ge(ready["biased"], s * HEADS - HEADS - 3)
                    turn(score[:, 0], lambda t: y2T[:, t * P:(t + 1) * P], "y2_p")
                if finish:
                    scores(7, s - 1, buf)
                if layers:
                    pe.wait_ge(ready["hT"], n)
                    for k in range(2):
                        last = pe.matmul(lc[:, k * N:(k + 1) * N], const("w1", k * P, P), hT[:], start=True, stop=True)
                    last.then_inc(ready["hid_p"], 1)
                if front:
                    pe.wait_ge(ready["loaded"], s * 64 + 128)
                    project(0, la)
                if finish:
                    weigh(6, s - 1)
                if layers:
                    pe.wait_ge(ready["hidT"], n2)
                    for t in range(T):
                        for k in range(2):
                            last = pe.matmul(lb[:, t * D:(t + 1) * D], hidT[:, k, t * P:(t + 1) * P], const("w2", k * D, D),
                                             start=k == 0, stop=k == 1)
                    last.then_inc(ready["out1_p"], 1)
                if finish:
                    weigh(7, s - 1)
                if attention:
                    pe.wait_ge(ready["x3"], s * 2)
                    turn(score[:, 0], lambda t: x3[:, 1 - buf, t], "x3_pT")
                if front:
                    pe.wait_ge(ready["loaded"], s * 64 + 128)
                    project(1, lc)
                if finish:
                    pe.wait_ge(ready["oT"], e)
                    for t in range(T):
                        for g in range(2):
                            last = pe.transpose(score[:, 1, (2 * t + g) * P:(2 * t + g + 1) * P], oT[:, g, t * P:(t + 1) * P], const("ident"))
                    last.then_inc(ready["o_p"], 1)
                if attention:
                    pe.wait_ge(ready["x3T"], m)
                    for t in range(T):
                        last = pe.matmul(att[:, t * D:(t + 1) * D], x3T[:, t * P:(t + 1) * P], const("wv"), start=True, stop=True)
                    last.then_inc(ready["v_p"], 1)
                    pe.wait_ge(ready["x3T_lo"], m)
                    project_heads(score[:, 0], "wq", "q_p")
                    pe.wait_ge(ready["x3T_lo"], m)
                    if finish:
                        pe.wait_ge(ready["o"], e)
                    project_heads(score[:, 1], "wk", "k_p")
                if finish:
                    pe.wait_ge(ready["o"], e)
                    turn(score[:, 2], lambda t: o[:, t], "o_pT")
                if layers:
                    if front:
                        pe.wait_ge(ready["gate_het"], s * 2 + 3)
                    pe.wait_ge(ready["x2"], n2)
                    turn(la, lambda t: x2[:, t], "x2_pT")
                if front:
                    pe.wait_ge(ready["hom_in"], s * 2 + 4)
                    if attention:
                        pe.wait_ge(ready["v_one"], m)
                    for t in range(T):
                        for k in range(T):
                            last = pe.matmul(att[:, t * D:(t + 1) * D], adjT_in[:, 1 - buf, k, t * P:(t + 1) * P], hom_in[:, k],
                                             start=k == 0, stop=k == T - 1)
                    last.then_inc(ready["agg0"], 1)
                if finish:
                    pe.wait_ge(ready["oT_all"], e)
                    for t in range(T):
                        last = pe.matmul(score[:, 2, N + t * D:N + (t + 1) * D], oT_all[:, t * P:(t + 1) * P], const("wo"), start=True, stop=True)
                    last.then_inc(ready["wo_p"], 1)
                if layers:
                    pe.wait_ge(ready["x2T"], n)
                    for t in range(T):
                        last = pe.matmul(la[:, t * D:(t + 1) * D], x2T[:, t * P:(t + 1) * P], const("wmsg"), start=True, stop=True)
                    last.then_inc(ready["msg_p"], 1)
                if attention:
                    pe.wait_ge(ready["masks"], s * 3)
                    pe.wait_ge(ready["q_lo"], m)
                    pe.wait_ge(ready["k_lo"], m)
                    scores_for_maxima(0)
                if layers:
                    pe.wait_ge(ready["x2T_lo"], n)
                    product(pe, lb[:, 0:N], "conv1", 0, (x2T_hi, x2T_lo)).then_inc(ready["conv1_p"], 1)
                    if front:
                        pe.wait_ge(ready["gate_het"], s * 2 + 4)
                    pe.wait_ge(ready["x2T_lo"], n)
                    product(pe, lc[:, 0:N], "wse", 0, (x2T_hi, x2T_lo)).then_inc(ready["se_p"], 1)
                if attention:
                    if finish:
                        pe.wait_ge(y_ready[3], e)
                    scores_for_maxima(1)
                if layers:
                    pe.wait_ge(ready["c1_hi"], n)
                    pe.wait_ge(ready["c1"], n)
                    conv2_pass(conv2_hi, c1_hi, first=True)
                if attention:
                    pe.wait_ge(ready["maxima"], s * 4 - 3)
                    scores_for_maxima(2)
                    pe.wait_ge(ready["maxima"], s * 4 - 2)
                    scores_for_maxima(3)
                if layers:
                    pe.wait_ge(ready["dist_dve"], n2)
                    pe.wait_ge(ready["dist_act"], n2)
                    for t in range(T):
                        last = pe.matmul(lc[:, t * N:(t + 1) * N], dist_l[0:96, t * P:(t + 1) * P], dist_r[0:96], start=True, stop=True)
                    last.then_inc(ready["dist_p"], 1)
                    conv2_pass(conv2_lo, c1_hi)
                if attention:
                    pe.wait_ge(ready["maxima"], s * 4)
                    if front:
                        pe.wait_ge(ready["hom_het"], s * 2 + 4)
                    turn(att, lambda t: maxima[:, t], "max_pT")
                if layers:
                    pe.wait_ge(ready["c1_lo"], n)
                    conv2_pass(conv2_hi, c1_lo, final=True)
                if attention:
                    pe.wait_ge(ready["shift"], s * 2)
                    pe.wait_ge(ready["q_copy"], m)
                    scores(0)
                    scores(1)
                if layers:
                    pe.wait_ge(ready["near"], n)
                    product(pe, lc[:, 0:N], "whh", 0, (x2T_hi, x2T_lo), stop=False)
                    pe.wait_ge(ready["msg"], n)
                    pe.wait_ge(ready["nearT"], n)
                    for k in range(T):
                        last = pe.matmul(la[:, 0:N], msg[:, k], nearT[:, k * N:(k + 1) * N], start=k == 0, stop=k == T - 1)
                    last.then_inc(ready["nmp_p"], 1)
                    pe.wait_ge(ready["conv_sum"], n)
                    product(pe, lb[:, N:2 * N], "whh", 2 * D, (x2T_hi, x2T_lo))
                if attention:
                    scores(2)
                    scores(3)
                if layers:
                    pe.wait_ge(ready["convT_lo"], n)
                    product(pe, lb[:, 0:N], "wih", 2 * D, (convT_hi, convT_lo), stop=False)
                if attention:
                    weigh(0)
                    weigh(1)
                if layers:
                    pe.wait_ge(ready["nmpT_lo"], n)
                    product(pe, lb[:, 0:N], "wih", 5 * D, (nmpT_hi, nmpT_lo), start=False).then_inc(ready["gn_p"], 1)
                    pe.wait_ge(ready["convT_lo"], n)
                    product(pe, lc[:, 0:N], "wih", 0, (convT_hi, convT_lo), start=False, stop=False)
                if attention:
                    scores(4)
                if layers:
                    pe.wait_ge(ready["nmpT_lo"], n)
                    product(pe, lc[:, 0:N], "wih", 3 * D, (nmpT_hi, nmpT_lo), start=False).then_inc(ready["r_p"], 1)
                    pe.wait_ge(ready["nmpT_lo"], n)
                    product(pe, la[:, 0:N], "whh", D, (x2T_hi, x2T_lo), stop=False)
                if attention:
                    weigh(2)
                    scores(5)
                if layers:
                    pe.wait_ge(ready["convT_lo"], n)
                    product(pe, la[:, 0:N], "wih", D, (convT_hi, convT_lo), start=False, stop=False)
                    pe.wait_ge(ready["nmpT_lo"], n)
                    product(pe, la[:, 0:N], "wih", 4 * D, (nmpT_hi, nmpT_lo), start=False).then_inc(ready["z_p"], 1)
                if attention:
                    scores(6)
                    weigh(3)
                    weigh(4)
                    weigh(5)

            first_step(body)
            pe.wait_ge(ready["setup_dve"], 1)
            pe.wait_ge(ready["we_ident"], HEADS)
            steps(pe, body)


def kernel(**inputs):
    import numpy as np
    import concourse.bacc as bacc
    from concourse.bass_utils import run_bass_kernel_spmd

    a = {name: np.asarray(v) for name, v in inputs.items()}

    def column(v, rows=P):
        return np.broadcast_to(v.reshape(1, -1), (rows, v.size))

    def columns(v, k):
        return v.reshape(k, P).T

    w_se, b_se = a["L2_gnn_w_se"], a["L2_gnn_b_se"]
    wse = np.zeros((D, P), w_se.dtype)
    bse = np.zeros((P, 1), b_se.dtype)
    for start in (0, 32, 64):
        wse[:, start:start + 3] = w_se.T
        bse[start:start + 3, 0] = b_se
    head_rows = np.zeros((P, GH), np.float32)
    shift_rows = np.zeros((P, HEADS), np.float32)
    for h in range(GH):
        for start in (0, HALF):
            head_rows[start + h * HD:start + (h + 1) * HD, h] = 1.0
    for h in range(HEADS):
        shift_rows[HALF + h, h] = 1.0
    twice = lambda w: np.concatenate([w[:, :HALF], w[:, :HALF], w[:, HALF:], w[:, HALF:]], 1)
    tiles = lambda w: np.concatenate(np.split(w, w.shape[0] // P, 0), 1)
    parts = {
        "w0": np.concatenate([a["L0_gnn_theta"], a["L0_gnn_W_h"], a["L0_gnn_W_t"]], 1),
        "w1": a["L1_gnn_W1"],
        "w2": tiles(a["L1_gnn_W2"]),
        "conv1": a["L2_gnn_conv1_w"][:, :, 0].T,
        "wmsg": a["L2_gnn_w_msg"].T,
        "wih": tiles(a["L2_gnn_w_ih"].T),
        "whh": a["L2_gnn_w_hh"].T,
        "wq": twice(a["L3_gnn_W_q"].T),
        "wk": twice(a["L3_gnn_W_k"].T),
        "wv": a["L3_gnn_W_v"].T,
        "wo": a["L3_gnn_W_o"].T,
        "wse": wse,
        "het_bt_row": column(np.concatenate([np.zeros(D, np.float32), a["L0_gnn_b_t"]])),
        "b2_row": column(a["L1_gnn_b2"]),
        "bmsg_row": column(a["L2_gnn_b_msg"]),
        "we": column(a["L3_gnn_W_e"]),
        "ident": np.eye(P, dtype=np.float32),
        "head_rows": head_rows,
        "shift_rows": shift_rows,
        "eps": column(a["L1_gnn_eps"]),
        "b1": columns(a["L1_gnn_b1"], 2),
        "bn1": np.stack([a[f"L2_gnn_bn1_{k}"] for k in "gbmv"], 1),
        "bn2": np.stack([a[f"L2_gnn_bn2_{k}"] for k in "gbmv"], 1),
        "bih": columns(a["L2_gnn_b_ih"], 3),
        "bhh": columns(a["L2_gnn_b_hh"], 3),
        "bse": bse,
    }
    arrays = {
        "x": a["x"],
        "xT": a["x"].transpose(0, 2, 1),
        "adj": a["adj"],
        "adjT": a["adj"].transpose(0, 2, 1),
        "packed": np.concatenate([parts[name] for name, _ in PARTS], 1),
        "conv2": a["L2_gnn_conv2_w"].transpose(1, 2, 0).reshape(D, TAPS * D),
    }
    arrays = {f"in_{name}": np.ascontiguousarray(v) for name, v in arrays.items()}
    nc = bacc.Bacc("TRN2", target_bir_lowering=False, num_devices=1)
    args = [nc.dram_tensor(name, v.shape, mybir.dt.from_np(v.dtype), kind="ExternalInput").ap() for name, v in arrays.items()]
    args.append(nc.dram_tensor("out", (BATCH, N, D), F32, kind="ExternalOutput").ap())
    gnn_stack_kernel(nc, *args)
    return run_bass_kernel_spmd(nc, [arrays], core_ids=[0]).results[0]["out"]
```
